# Optimizing a Trainium2 kernel written in Bass

```python
import numpy as np
import jax
import jax.numpy as jnp

def _softmax(x, axis=-1):
    return jax.nn.softmax(x, axis=axis)

def _gelu(x):
    return jax.nn.gelu(x, approximate=True)

def _silu(x):
    return jax.nn.silu(x)

def _sigmoid(x):
    return jax.nn.sigmoid(x)

def _layernorm(x, axis=-1, eps=1e-05):
    m = jnp.mean(x, axis=axis, keepdims=True)
    v = jnp.var(x, axis=axis, keepdims=True)
    return (x - m) / jnp.sqrt(v + eps)

def _scatter_add(tgt, idx, src, axis=0):
    return tgt.at[idx].add(src)

def _segment_sum(src, seg, n):
    return jax.ops.segment_sum(src, seg, n)
kernel_name = 'mk_gnn_resnorm_d1_gnn_r8_dae6a2'

def setup_inputs(seed: int=0):
    np.random.seed(seed)
    _w = jnp.asarray

    def _rec_inputs():
        import jax
        import jax.numpy as jnp
        _gk = jax.random.key(seed)
        x = -0.0005121 + 1.001 * jax.random.normal(jax.random.fold_in(_gk, 1), (6250, 64), jnp.float32)
        _s = jax.random.randint(jax.random.fold_in(_gk, 2), (100000,), 0, 6250, jnp.int32)
        _d = jax.random.randint(jax.random.fold_in(_gk, 3), (100000,), 0, 6250, jnp.int32)
        _loop = jnp.arange(6250, dtype=jnp.int32)
        src = jnp.concatenate([_s, _d, _loop])
        dst = jnp.concatenate([_d, _s, _loop])
        _o = jnp.argsort(dst, stable=True)
        src = src[_o]
        dst = dst[_o]
        return (x, src, dst)
    x, src, dst = _rec_inputs()

    def _L0_gnn_setup():
        import jax, jax.numpy as jnp
        import numpy as np
        N = 6250
        E = 100000
        IN_NF = 64
        HID = 128
        OUT_NF = 64
        L = 4
        EH = HID // 2
        C = 1.0

        def _w(k, shape):
            return jax.random.normal(k, shape, dtype=jnp.float32) / np.sqrt(shape[-2]).astype(np.float32)
        key = jax.random.key(seed)
        ks = jax.random.split(key, 10)
        h = jax.random.normal(ks[0], (N, IN_NF), dtype=jnp.float32)
        edges = jax.random.randint(ks[1], (2, E), 0, N, dtype=jnp.int32)
        return {'h': h, 'edges': edges, 'W_in': _w(ks[2], (IN_NF, HID)), 'b_in': jnp.zeros((HID,), jnp.float32), 'eW1': _w(ks[3], (L, 2 * HID, EH)), 'eb1': jnp.zeros((L, EH), jnp.float32), 'eW2': _w(ks[4], (L, EH, EH)), 'eb2': jnp.zeros((L, EH), jnp.float32), 'nW1': _w(ks[5], (L, HID + EH, HID)), 'nb1': jnp.zeros((L, HID), jnp.float32), 'nW2': _w(ks[6], (L, HID, HID)), 'nb2': jnp.zeros((L, HID), jnp.float32), 'W_out': _w(ks[7], (HID, OUT_NF)), 'b_out': jnp.zeros((OUT_NF,), jnp.float32)}
    _L0_gnn_all = _L0_gnn_setup()
    _L0_gnn_in = {k: v for k, v in _L0_gnn_all.items() if k in ('W_in', 'b_in', 'eW1', 'eb1', 'eW2', 'eb2', 'nW1', 'nb1', 'nW2', 'nb2', 'W_out', 'b_out')}
    del _L0_gnn_all
    return {'x': x, 'src': src, 'dst': dst, 'L0_gnn_W_in': _L0_gnn_in['W_in'], 'L0_gnn_b_in': _L0_gnn_in['b_in'], 'L0_gnn_eW1': _L0_gnn_in['eW1'], 'L0_gnn_eb1': _L0_gnn_in['eb1'], 'L0_gnn_eW2': _L0_gnn_in['eW2'], 'L0_gnn_eb2': _L0_gnn_in['eb2'], 'L0_gnn_nW1': _L0_gnn_in['nW1'], 'L0_gnn_nb1': _L0_gnn_in['nb1'], 'L0_gnn_nW2': _L0_gnn_in['nW2'], 'L0_gnn_nb2': _L0_gnn_in['nb2'], 'L0_gnn_W_out': _L0_gnn_in['W_out'], 'L0_gnn_b_out': _L0_gnn_in['b_out']}

def reference(x, src, dst, L0_gnn_W_in, L0_gnn_b_in, L0_gnn_eW1, L0_gnn_eb1, L0_gnn_eW2, L0_gnn_eb2, L0_gnn_nW1, L0_gnn_nb1, L0_gnn_nW2, L0_gnn_nb2, L0_gnn_W_out, L0_gnn_b_out):
    import jax
    import jax.numpy as jnp

    def _L0_gnn_ref(h, edges, W_in, b_in, eW1, eb1, eW2, eb2, nW1, nb1, nW2, nb2, W_out, b_out):
        import jax, jax.numpy as jnp
        import numpy as np
        N = 6250
        E = 100000
        IN_NF = 64
        HID = 128
        OUT_NF = 64
        L = 4
        EH = HID // 2
        C = 1.0

        def _w(k, shape):
            return jax.random.normal(k, shape, dtype=jnp.float32) / np.sqrt(shape[-2]).astype(np.float32)
        row, col = (edges[0], edges[1])
        h = h @ W_in + b_in

        def layer(hc, p):
            w1, b1, w2, b2, m1, c1, m2, c2 = p
            m = jnp.concatenate([hc[row], hc[col]], axis=1)
            m = jax.nn.silu(m @ w1 + b1)
            m = jax.nn.silu(m @ w2 + b2)
            agg = jax.ops.segment_sum(m, row, num_segments=N) * C
            z = jnp.concatenate([hc, agg], axis=1)
            z = jax.nn.silu(z @ m1 + c1)
            z = z @ m2 + c2
            return (hc + z, None)
        h, _ = jax.lax.scan(layer, h, (eW1, eb1, eW2, eb2, nW1, nb1, nW2, nb2))
        return h @ W_out + b_out
    edge_index = jnp.stack([src, dst])
    x = _layernorm(x + _L0_gnn_ref(x, edge_index, L0_gnn_W_in, L0_gnn_b_in, L0_gnn_eW1, L0_gnn_eb1, L0_gnn_eW2, L0_gnn_eb2, L0_gnn_nW1, L0_gnn_nb1, L0_gnn_nW2, L0_gnn_nb2, L0_gnn_W_out, L0_gnn_b_out), axis=-1)
    return x

_drawn_inputs = setup_inputs


def setup_inputs(seed=0):
    import zlib

    import numpy as np

    out = dict(_drawn_inputs(seed))
    spreads = {'L0_gnn_b_in': (0.0, 0.1),
     'L0_gnn_eb1': (0.0, 0.1),
     'L0_gnn_eb2': (0.0, 0.1),
     'L0_gnn_nb1': (0.0, 0.634),
     'L0_gnn_nb2': (0.0, 0.465),
     'L0_gnn_b_out': (0.0, 0.8)}
    factors = {}
    for name, (base, spread) in spreads.items():
        noise = np.random.default_rng([zlib.crc32(name.encode()), seed]).standard_normal(out[name].shape)
        drawn = base * np.exp(spread * noise) if base else spread * noise
        out[name] = jnp.asarray(drawn.astype(out[name].dtype))
    for name, factor in factors.items():
        out[name] = (out[name] * factor).astype(out[name].dtype)
    return out
```

```python
import concourse.bass as bass
from concourse import mybir
from contextlib import ExitStack

F32 = mybir.dt.float32
BF16 = mybir.dt.bfloat16
I32 = mybir.dt.int32
U16 = mybir.dt.uint16
ALU = mybir.AluOpType
ACT = mybir.ActivationFunctionType
AX = mybir.AxisListType
DVE_ONLY = [mybir.EngineType.DVE]
ACT_ONLY = [mybir.EngineType.Activation]

P = 128
TPP = 2
PPQ = 4
TPQ = TPP * PPQ
DMA = 16


def divisor(n, most, even_count=False):
    return max(d for d in range(1, most + 1) if n % d == 0 and not (even_count and (n // d) % 2))


def build_gnn(nc, x, src, dst, W_in, b_in, eW1, eb1, eW2, eb2, nW1, nb1, nW2, nb2, W_out, b_out, out):
    N, F = x.shape
    E = src.shape[0]
    H = W_in.shape[1]
    L, _, EH = eW1.shape
    assert H == P and EH * 2 == P and F == EH
    NB = -(-N // P)
    NP = NB * P
    NC = -(-E // P)
    EP = NC * P
    SB = divisor(NC, 32, even_count=True)
    NPAIR = (EP + NB * (TPP * P - 1)) // (TPP * P)
    NQ = -(-NPAIR // PPQ)
    NQ += NQ % 2
    NPAIR = NQ * PPQ
    T = NQ * TPQ
    CH = divisor(NP, 512, even_count=True)
    NCH = NP // CH
    GT = divisor(NB, 7)
    NG = NB // GT
    RB = divisor(T, P)
    NRB = T // RB

    records = nc.dram_tensor("records", (P * T, 2), I32).ap()
    recv_rows = nc.dram_tensor("recv_rows", (T, P), BF16).ap()
    dst_table = nc.dram_tensor("dst_table", (NP, EH), F32).ap()

    with ExitStack() as ctx:
        def sb(name, shape, dt, c=ctx):
            return c.enter_context(nc.sbuf_tensor(name, shape, dt))

        def sem(name):
            return ctx.enter_context(nc.semaphore(name))

        ident = sb("ident", [P, P], F32)
        ident_b = sb("ident_b", [P, P], BF16)
        tri = sb("tri", [P, P], F32)
        ones = sb("ones", [P, P], F32)
        ones_b = sb("ones_b", [P, P], BF16)
        part = sb("part", [P, 1], F32)
        lane = sb("lane", [P, P], F32)
        bucket_no = sb("bucket_no", [P, NB], F32)
        pick3 = sb("pick3", [P, 3], F32)

        W_in_sb = sb("W_in_sb", [F, H], F32)
        b_in_sb = sb("b_in_sb", [H, 1], F32)
        w1_sb = sb("w1_sb", [H, 2 * EH], F32)
        b1_bc = sb("b1_bc", [P, EH], F32)
        w2_sb = sb("w2_sb", [P, P], F32)
        b2_bc = sb("b2_bc", [P, EH], F32)
        b2_hi = sb("b2_hi", [P, EH], BF16)
        b2_mid = sb("b2_mid", [P, EH], BF16)
        b2_r1 = sb("b2_r1", [P, EH], F32)
        b2_r2 = sb("b2_r2", [P, EH], F32)
        b2_sum = sb("b2_sum", [P, EH], F32)
        b2_parts = sb("b2_parts", [P, TPQ, EH], BF16)
        m1h_sb = sb("m1h_sb", [H, H], F32)
        m1a_sb = sb("m1a_sb", [EH, H], F32)
        c1_sb = sb("c1_sb", [H, 1], F32)
        m2_sb = sb("m2_sb", [H, H], F32)
        c2_sb = sb("c2_sb", [H, 1], F32)
        W_out_sb = sb("W_out_sb", [H, F], F32)
        b_out_bc = sb("b_out_bc", [P, F], F32)

        hT = sb("hT", [H, NP], F32)
        aggT = sb("aggT", [EH, NP], F32)
        xT = aggT
        node_sb = sb("node_sb", [P, NB, EH], F32)
        dst_idx = sb("dst_idx", [P, T], I32)
        recv = sb("recv", [P, T], F32)
        pair_bucket = sb("pair_bucket", [P, NPAIR], I32)
        pair_f = sb("pair_f", [P, NPAIR], F32)
        pair_no = sb("pair_no", [P, NPAIR], F32)
        recs = sb("recs", [P, T, 2], I32)

        with ExitStack() as early:
            recs_in = sb("recs_in", [P, NC, 2], I32, early)
            src_raw = sb("src_raw", [P, NC], I32, early)
            dst_raw = sb("dst_raw", [P, NC], I32, early)
            bkt_i = sb("bkt_i", [P, NC], I32, early)
            bkt = sb("bkt", [P, NC], BF16, early)
            mask = sb("mask", [P, NC], BF16, early)
            ones_row = sb("ones_row", [P, NC], BF16, early)
            scan = sb("scan", [P, NC], F32, early)
            rank = sb("rank", [P, NC], F32, early)
            rank_i = sb("rank_i", [P, NC], I32, early)
            slot_lo = sb("slot_lo", [P, NC], I32, early)
            slot_hi = sb("slot_hi", [P, NC], I32, early)
            pos = sb("pos", [P, NC], I32, early)
            cnt = sb("cnt", [P, NB], F32, early)
            tot_i = sb("tot_i", [P, NB], I32, early)
            npair_i = sb("npair_i", [P, NB], I32, early)
            npair = sb("npair", [P, NB], F32, early)
            pair_end = sb("pair_end", [P, NB], F32, early)
            first = sb("first", [P, NB], F32, early)
            pos_stage = sb("pos_stage", [P, 2, SB], I32, early)
            rec_stage = sb("rec_stage", [P, 2, SB, 2], I32, early)
        with ExitStack() as mid:
            recv_b = sb("recv_b", [P, T], BF16, mid)
            recv_t = sb("recv_t", [RB, NRB, P], BF16, mid)

        agg = sb("agg", [P, NB, EH], F32)
        src_table = sb("src_table", [P, NB, 3, EH], BF16)
        tab_r1 = sb("tab_r1", [P, 2, GT, EH], F32)
        recv_bc = sb("recv_bc", [P, 2, TPQ * P], BF16)
        pick = sb("pick", [P, 2, TPQ * P], BF16)
        pick_t = sb("pick_t", [P, 2, TPQ, P], F32)
        src_rows = sb("src_rows", [P, 2, PPQ, 3, EH], BF16)
        idx_stage = sb("idx_stage", [P, 2, TPQ], I32)
        gath = sb("gath", [P, 2, TPQ * EH], F32)
        s1 = sb("s1", [P, 2, PPQ * P], F32)
        msg = sb("msg", [P, 2, TPQ, EH], F32)
        u_sb = sb("u_sb", [H, 2, CH], F32)
        y = agg
        sq = sb("sq", [P, NB, EH], F32)
        stat = sb("stat", [P, 4, NB], F32)

        psum = ctx.enter_context(nc.psum_tensor("psum", [P, 8, 512], F32))
        pre_ps = psum[:, 0:2, :]
        z_ps = psum[:, 2:4, :]
        agg_ps = psum[:, 4:6, :]
        grp_ps = [psum[:, 0:2, :].rearrange("p b c -> p (b c)"), psum[:, 2:4, :].rearrange("p b c -> p (b c)")]
        cnt_ps = psum[:, 6, :]
        rt_ps = psum[:, 4:8, :].rearrange("p b c -> p (b c)")

        x_zero = sem("x_zero")
        loaded = sem("loaded")
        edges_in = sem("edges_in")
        consts = sem("consts")
        padded = sem("padded")
        pad_set = sem("pad_set")
        turn = sem("turn")
        seq = sem("seq")
        summed = sem("summed")
        count_step = sem("count_step")
        pair_step = sem("pair_step")
        rank_step = sem("rank_step")
        staged = [sem("staged0"), sem("staged1")]
        scattered = [sem("scattered0"), sem("scattered1")]
        recs_back = sem("recs_back")
        recv_ready = sem("recv_ready")
        recv_tr = sem("recv_tr")
        recv_copied = sem("recv_copied")
        recv_out = sem("recv_out")
        sorted_ = sem("sorted")
        x_tr = sem("x_tr")
        x_tr_out = sem("x_tr_out")
        h0_ps = sem("h0_ps")
        h0_out = sem("h0_out")
        weights = sem("weights")
        b2_ready = sem("b2_ready")
        tab_ps = sem("tab_ps")
        tab_hi = sem("tab_hi")
        tab_r = sem("tab_r")
        tab_mid = sem("tab_mid")
        tab_done = sem("tab_done")
        table_out = sem("table_out")
        agg_zero = sem("agg_zero")
        b2_step = sem("b2_step")
        bc_ready = [sem("bc_ready0"), sem("bc_ready1")]
        pick_ready = [sem("pick_ready0"), sem("pick_ready1")]
        pick_t_ready = [sem("pick_t_ready0"), sem("pick_t_ready1")]
        rows_ready = [sem("rows_ready0"), sem("rows_ready1")]
        idx_ready = [sem("idx_ready0"), sem("idx_ready1")]
        gathered = [sem("gathered0"), sem("gathered1")]
        pre_ready = [sem("pre_ready0"), sem("pre_ready1")]
        s1_ready = [sem("s1_ready0"), sem("s1_ready1")]
        z_ready = [sem("z_ready0"), sem("z_ready1")]
        msg_ready = [sem("msg_ready0"), sem("msg_ready1")]
        agg_ready = [sem("agg_ready0"), sem("agg_ready1")]
        added = [sem("added0"), sem("added1")]
        agg_tr = sem("agg_tr")
        aggT_ready = sem("aggT_ready")
        u_ps_ready = [sem("u_ps_ready0"), sem("u_ps_ready1")]
        u_ready = [sem("u_ready0"), sem("u_ready1")]
        upd_ps = [sem("upd_ps0"), sem("upd_ps1")]
        h_ready = sem("h_ready")
        x_back = sem("x_back")
        o_ps = sem("o_ps")
        o_out = sem("o_out")
        o_ready = sem("o_ready")
        fin_step = sem("fin_step")
        sqrt_done = sem("sqrt_done")
        stored = sem("stored")

        NTAIL = N - (NB - 1) * P
        CTAIL = E - (P - 1) * NC
        assert 0 < CTAIL <= NC
        N_LOADED = 4 + (2 if NB > 1 else 1)
        N_WEIGHTS = 11
        N_CONSTS = 7
        HQ = NQ // 2
        HCH = NCH // 2
        assert NRB * P <= 2048 and NQ % 2 == 0 and GT * P <= 1024

        block = ctx.enter_context(nc.Block())

        def x_loads(eng, s):
            if NB > 1:
                eng.dma_start(node_sb[:, 0:NB - 1, :],
                              x[0:(NB - 1) * P, :].rearrange("(i p) f -> p i f", p=P)).then_inc(s, DMA)
            eng.dma_start(node_sb[0:NTAIL, NB - 1, :], x[(NB - 1) * P:N, :]).then_inc(s, DMA)

        @block.sync
        def _(sp):
            sp.wait_ge(x_zero, 1)
            x_loads(sp, loaded)
            sp.dma_start(W_in_sb[:, :], W_in).then_inc(loaded, DMA)
            sp.dma_start(b_in_sb[:, :], b_in.rearrange("(h o) -> h o", o=1)).then_inc(loaded, DMA)
            sp.dma_start(W_out_sb[:, :], W_out).then_inc(loaded, DMA)
            sp.dma_start(b_out_bc[:, :], b_out.partition_broadcast(P)).then_inc(loaded, DMA)
            for s in range(2):
                sp.wait_ge(scattered[s], DMA * (NC // 2))
            sp.dma_start(recs[:, :, :], records.rearrange("(p t) c -> p t c", p=P)).then_inc(recs_back, DMA)
            sp.wait_ge(recv_copied, 1)
            sp.dma_start(recv_rows.rearrange("(b r) p -> r b p", r=RB), recv_t[:, :, :]).then_inc(recv_out, DMA)
            sp.wait_ge(recv_out, DMA)
            with sp.Fori(0, L) as l:
                sp.wait_ge(h_ready, (l + 1) * NCH)
                dl = bass.ds(l, 1)
                sp.dma_start(w1_sb[:, 0:EH], eW1[dl, 0:H, :].rearrange("o h e -> (o h) e")).then_inc(weights, DMA)
                sp.dma_start(w1_sb[:, EH:P], eW1[dl, H:2 * H, :].rearrange("o h e -> (o h) e")).then_inc(weights, DMA)
                sp.dma_start(b1_bc[:, :], eb1[dl, :].rearrange("o e -> (o e)").partition_broadcast(P)).then_inc(weights, DMA)
                sp.dma_start(w2_sb[0:EH, 0:EH], eW2[dl, :, :].rearrange("o h e -> (o h) e")).then_inc(weights, DMA)
                sp.dma_start(w2_sb[EH:P, EH:P], eW2[dl, :, :].rearrange("o h e -> (o h) e")).then_inc(weights, DMA)
                sp.dma_start(b2_bc[:, :], eb2[dl, :].rearrange("o e -> (o e)").partition_broadcast(P)).then_inc(weights, DMA)
                sp.dma_start(m1h_sb[:, :], nW1[dl, 0:H, :].rearrange("o h e -> (o h) e")).then_inc(weights, DMA)
                sp.dma_start(m1a_sb[:, :], nW1[dl, H:H + EH, :].rearrange("o h e -> (o h) e")).then_inc(weights, DMA)
                sp.dma_start(m2_sb[:, :], nW2[dl, :, :].rearrange("o h e -> (o h) e")).then_inc(weights, DMA)
                sp.dma_start(c1_sb[:, :], nb1[dl, :].rearrange("o h -> h o")).then_inc(weights, DMA)
                sp.dma_start(c2_sb[:, :], nb2[dl, :].rearrange("o h -> h o")).then_inc(weights, DMA)
                sp.wait_ge(tab_done, (l + 1) * NG)
                sp.dma_start(dst_table.rearrange("(i p) e -> p i e", p=P), node_sb[:, :, :]).then_inc(table_out, DMA)
                with sp.Fori(0, HQ) as j:
                    for s in range(2):
                        it = l * HQ + j
                        sp.wait_ge(pick_ready[s], it)
                        sp.dma_start(recv_bc[:, s, :],
                                     recv_rows[bass.ds((2 * j + s) * TPQ, TPQ), :]
                                     .rearrange("t p -> (t p)").partition_broadcast(P)).then_inc(bc_ready[s], DMA)
            sp.wait_ge(table_out, DMA * L)
            x_loads(sp, x_back)
            sp.wait_ge(o_ready, 1)
            if NB > 1:
                sp.dma_start(out[0:(NB - 1) * P, :].rearrange("(i p) f -> p i f", p=P),
                             y[:, 0:NB - 1, :]).then_inc(stored, DMA)
            sp.dma_start(out[(NB - 1) * P:N, :], y[0:NTAIL, NB - 1, :]).then_inc(stored, DMA)
            sp.wait_ge(stored, DMA * (2 if NB > 1 else 1))

        @block.gpsimd
        def _(pool):
            nc.gpsimd.memset(node_sb[:, NB - 1, :], 0.0).then_inc(x_zero, 1)
            nc.gpsimd.iota(lane[:, :], [[1, P]], base=0, channel_multiplier=0,
                           allow_small_or_imprecise_dtypes=True).then_inc(consts, 1)
            nc.gpsimd.iota(part[:, :], [[1, 1]], base=0, channel_multiplier=1,
                           allow_small_or_imprecise_dtypes=True).then_inc(consts, 1)
            nc.gpsimd.iota(bucket_no[:, :], [[1, NB]], base=0, channel_multiplier=0,
                           allow_small_or_imprecise_dtypes=True).then_inc(consts, 1)
            nc.gpsimd.memset(w2_sb[:, :], 0.0).then_inc(consts, 1)
            nc.gpsimd.iota(pair_no[:, :], [[1, NPAIR]], base=0, channel_multiplier=0,
                           allow_small_or_imprecise_dtypes=True).then_inc(consts, 1)
            nc.gpsimd.memset(src_raw[:, :], NP - 1).then_inc(consts, 1)
            nc.gpsimd.memset(dst_raw[:, :], 0).then_inc(consts, 1)
            nc.gpsimd.memset(recs[:, :, 0], -1).then_inc(pad_set, 1)
            nc.gpsimd.memset(recs[:, :, 1], 0).then_inc(pad_set, 1)
            pool.wait_ge(pad_set, 2)
            pool.dma_start(records.rearrange("(p t) c -> p t c", p=P), recs[:, :, :]).then_inc(padded, DMA)
            pool.wait_ge(padded, DMA)
            with pool.Fori(0, NC // SB // 2) as j:
                for s in range(2):
                    pool.wait_ge(staged[s], 2 * (j + 1))
                    pool.sem_inc(turn, 1)
                    for c in range(SB):
                        nc.gpsimd.indirect_dma_start(
                            out=records, out_offset=bass.IndirectOffsetOnAxis(ap=pos_stage[:, s, c:c + 1], axis=0),
                            in_=rec_stage[:, s, c, :], in_offset=None).then_inc(scattered[s], DMA)
            with pool.Fori(0, L) as l:
                pool.wait_ge(table_out, DMA * (l + 1))
                pool.sem_inc(turn, 1)
                with pool.Fori(0, HQ) as j:
                    for s in range(2):
                        it = l * HQ + j
                        pool.wait_ge(idx_ready[s], it + 1)
                        pool.wait_ge(pre_ready[s], it)
                        pool.sem_inc(turn, 1)
                        for t in range(TPQ):
                            nc.gpsimd.indirect_dma_start(
                                out=gath[:, s, t * EH:(t + 1) * EH], out_offset=None, in_=dst_table,
                                in_offset=bass.IndirectOffsetOnAxis(ap=idx_stage[:, s, t:t + 1], axis=0),
                            ).then_inc(gathered[s], DMA)

        @block.vector
        def _(v):
            n_seq = [0]

            def step(ins):
                n_seq[0] += 1
                ins.then_inc(seq, 1)
                v.wait_ge(seq, n_seq[0])

            V = nc.vector
            v.wait_ge(consts, N_CONSTS)
            step(V.tensor_scalar(ident[:, :], lane[:, :], part[:, 0:1], None, ALU.is_equal))
            step(V.tensor_copy(ident_b[:, :], ident[:, :]))
            step(V.tensor_scalar(tri[:, :], lane[:, :], part[:, 0:1], None, ALU.is_gt))
            step(V.memset(ones[:, :], 1.0))
            step(V.memset(ones_b[:, :], 1.0))
            step(V.memset(ones_row[:, :], 1.0))
            step(V.tensor_scalar(pick3[:, :], lane[:, 0:3], part[:, 0:1], None, ALU.is_equal))

            v.wait_ge(edges_in, DMA * 4)
            step(V.tensor_scalar(bkt_i[:, :], src_raw[:, :], 7, None, ALU.logical_shift_right))
            step(V.tensor_copy(bkt[:, :], bkt_i[:, :]))
            step(V.tensor_copy(recs_in[:, :, 0], src_raw[:, :]))
            step(V.tensor_copy(recs_in[:, :, 1], dst_raw[:, :]))
            with v.Fori(0, NB) as b:
                v.wait_ge(count_step, b)
                V.tensor_scalar(mask[:, :], bkt[:, :], bucket_no[:, bass.ds(b, 1)], 0.0, ALU.is_equal, ALU.add,
                                accum_out=cnt[:, bass.ds(b, 1)]).then_inc(count_step, 1)
            v.wait_ge(summed, 2)
            step(V.tensor_copy(tot_i[:, :], cnt_ps[:, NB:2 * NB]))
            step(V.tensor_scalar(tot_i[:, :], tot_i[:, :], TPP * P - 1, None, ALU.add))
            step(V.tensor_scalar(npair_i[:, :], tot_i[:, :], 8, None, ALU.logical_shift_right))
            step(V.tensor_copy(npair[:, :], npair_i[:, :]))
            step(V.tensor_tensor_scan(pair_end[:, :], ones[:, 0:NB], npair[:, :], 0.0, ALU.mult, ALU.add))
            step(V.tensor_tensor(first[:, :], pair_end[:, :], npair[:, :], ALU.subtract))
            step(V.tensor_scalar(first[:, :], first[:, :], float(TPP * P), -1.0, ALU.mult, ALU.add))
            step(V.tensor_tensor(first[:, :], first[:, :], cnt_ps[:, 0:NB], ALU.add))
            with v.Fori(0, NB) as b:
                v.wait_ge(rank_step, 3 * b)
                V.tensor_scalar(mask[:, :], bkt[:, :], bucket_no[:, bass.ds(b, 1)], None,
                                ALU.is_equal).then_inc(rank_step, 1)
                v.wait_ge(rank_step, 3 * b + 1)
                V.tensor_tensor_scan(scan[:, :], ones_row[:, :], mask[:, :], first[:, bass.ds(b, 1)],
                                     ALU.mult, ALU.add).then_inc(rank_step, 1)
                v.wait_ge(rank_step, 3 * b + 2)
                v.sem_inc(turn, 1)
                V.copy_predicated(rank[:, :], mask[:, :].bitcast(U16), scan[:, :]).then_inc(rank_step, 1)
            v.wait_ge(rank_step, 3 * NB)
            step(V.tensor_copy(rank_i[:, :], rank[:, :]))
            step(V.tensor_scalar(slot_lo[:, :], rank_i[:, :], P - 1, None, ALU.bitwise_and))
            step(V.tensor_scalar(slot_hi[:, :], rank_i[:, :], 7, None, ALU.logical_shift_right))
            step(V.scalar_tensor_tensor(pos[:, :], slot_lo[:, :], float(T), slot_hi[:, :], ALU.mult, ALU.add))
            with v.Fori(0, NC // SB // 2) as j:
                for s in range(2):
                    v.wait_ge(scattered[s], DMA * SB * j)
                    c0 = (2 * j + s) * SB
                    V.tensor_copy(pos_stage[:, s, :], pos[:, bass.ds(c0, SB)]).then_inc(staged[s], 1)
                    V.tensor_copy(rec_stage[:, s, :, :], recs_in[:, bass.ds(c0, SB), :]).then_inc(staged[s], 1)

            step(V.memset(pair_f[:, :], 0.0))
            with v.Fori(0, NB - 1) as b:
                v.wait_ge(pair_step, b)
                V.scalar_tensor_tensor(pair_f[:, :], pair_no[:, :], pair_end[:, bass.ds(b, 1)], pair_f[:, :],
                                       ALU.is_ge, ALU.add).then_inc(pair_step, 1)
            v.wait_ge(pair_step, NB - 1)
            step(V.tensor_copy(pair_bucket[:, :], pair_f[:, :]))
            v.wait_ge(recs_back, DMA)
            step(V.tensor_copy(dst_idx[:, :], recs[:, :, 1]))
            step(V.tensor_copy(recv[:, :], recs[:, :, 0]))
            step(V.scalar_tensor_tensor(recv[:, :].rearrange("p (a b) -> p a b", b=TPP),
                                        pair_f[:, :].unsqueeze(2).to_broadcast([P, NPAIR, TPP]), -float(P),
                                        recv[:, :].rearrange("p (a b) -> p a b", b=TPP), ALU.mult, ALU.add))
            V.tensor_copy(recv_b[:, :], recv[:, :]).then_inc(recv_ready, 1)
            v.wait_ge(recv_tr, 1)
            V.tensor_copy(recv_t[:, :, :].rearrange("r b p -> r (b p)"), rt_ps[0:RB, 0:NRB * P]).then_inc(recv_copied, 1)
            v.wait_ge(recv_out, DMA)
            V.memset(b2_parts[:, :, :], 0.0).then_inc(sorted_, 1)

            with v.Fori(0, L) as l:
                v.wait_ge(agg_tr, l * NG)
                v.wait_ge(sorted_, 1)
                V.memset(agg[:, :, :], 0.0).then_inc(agg_zero, 1)
                v.wait_ge(weights, DMA * N_WEIGHTS * (l + 1))
                v.wait_ge(z_ready[1], l * HQ)
                B2 = 8
                V.tensor_copy(b2_hi[:, :], b2_bc[:, :]).then_inc(b2_step, 1)
                v.wait_ge(b2_step, l * B2 + 1)
                V.tensor_tensor(b2_r1[:, :], b2_bc[:, :], b2_hi[:, :], ALU.subtract).then_inc(b2_step, 1)
                v.wait_ge(b2_step, l * B2 + 2)
                V.tensor_copy(b2_mid[:, :], b2_r1[:, :]).then_inc(b2_step, 1)
                v.wait_ge(b2_step, l * B2 + 3)
                V.tensor_tensor(b2_r2[:, :], b2_r1[:, :], b2_mid[:, :], ALU.subtract).then_inc(b2_step, 1)
                v.wait_ge(b2_step, l * B2 + 4)
                V.tensor_scalar(b2_sum[:, :], b2_hi[:, :], pick3[:, 0:1], None, ALU.mult).then_inc(b2_step, 1)
                v.wait_ge(b2_step, l * B2 + 5)
                V.scalar_tensor_tensor(b2_sum[:, :], b2_mid[:, :], pick3[:, 1:2], b2_sum[:, :],
                                       ALU.mult, ALU.add).then_inc(b2_step, 1)
                v.wait_ge(b2_step, l * B2 + 6)
                V.scalar_tensor_tensor(b2_sum[:, :], b2_r2[:, :], pick3[:, 2:3], b2_sum[:, :],
                                       ALU.mult, ALU.add).then_inc(b2_step, 1)
                v.wait_ge(b2_step, l * B2 + 7)
                V.tensor_copy(b2_parts[:, :, :], b2_sum[:, :].unsqueeze(1).to_broadcast([P, TPQ, EH])).then_inc(b2_step, 1)
                v.wait_ge(table_out, DMA * l)
                for g in range(NG):
                    s, at = g % 2, slice(g * GT, (g + 1) * GT)
                    ps = grp_ps[s][:, 0:GT * P].rearrange("p (i c) -> p i c", c=P)
                    v.wait_ge(tab_hi, l * NG + g + 1)
                    V.tensor_tensor(tab_r1[:, s, :, :], ps[:, :, 0:EH], src_table[:, at, 0, :],
                                    ALU.subtract).then_inc(tab_r, 1)
                    V.tensor_tensor(node_sb[:, at, :], ps[:, :, EH:P],
                                    b1_bc[:, :].unsqueeze(1).to_broadcast([P, GT, EH]), ALU.add).then_inc(tab_done, 1)
                    v.wait_ge(tab_r, 3 * (l * NG + g) + 1)
                    V.tensor_copy(src_table[:, at, 1, :], tab_r1[:, s, :, :]).then_inc(tab_r, 1)
                    v.wait_ge(tab_r, 3 * (l * NG + g) + 2)
                    V.tensor_tensor(src_table[:, at, 2, :], tab_r1[:, s, :, :], src_table[:, at, 1, :],
                                    ALU.subtract).then_inc(tab_r, 1)
                v.wait_ge(agg_zero, l + 1)

                def prepare(q, it, s):
                    v.wait_ge(bc_ready[s], DMA * (it + 1))
                    v.wait_ge(pre_ready[s], it)
                    V.tensor_scalar(pick[:, s, :], recv_bc[:, s, :], part[:, 0:1], None,
                                    ALU.is_equal).then_inc(pick_ready[s], 1)
                    v.wait_ge(agg_ready[s], it)
                    V.tensor_tensor(pick_t[:, s, :, :], lane[:, :].unsqueeze(1).to_broadcast([P, TPQ, P]),
                                    recv[:, bass.ds(q * TPQ, TPQ)].unsqueeze(2).to_broadcast([P, TPQ, P]),
                                    ALU.is_equal).then_inc(pick_t_ready[s], 1)

                def add(q, it, s):
                    _, bucket = nc.values_load_multi_w_load_instructions(
                        pair_bucket[0:1, bass.ds(q * PPQ, PPQ)], engines=DVE_ONLY, min_val=0, max_val=NB - 1,
                        skip_runtime_bounds_check_because="a count of buckets that end before is 0 to NB - 1")
                    v.wait_ge(agg_ready[s], it + 1)
                    for k in range(PPQ):
                        if k:
                            v.wait_ge(added[s], it * PPQ + k)
                        else:
                            v.wait_ge(added[1 - s], (it + s) * PPQ)
                        where = agg[:, bass.ds(bucket[k], 1), :].rearrange("p o e -> p (o e)")
                        V.tensor_tensor(where, where, agg_ps[:, s, k * EH:(k + 1) * EH], ALU.add).then_inc(added[s], 1)

                prepare(0, l * HQ, 0)
                if HQ > 1:
                    with v.Fori(0, HQ - 1) as j:
                        prepare(2 * j + 1, l * HQ + j, 1)
                        add(2 * j, l * HQ + j, 0)
                        prepare(2 * j + 2, l * HQ + j + 1, 0)
                        add(2 * j + 1, l * HQ + j, 1)
                prepare(NQ - 1, l * HQ + HQ - 1, 1)
                add(NQ - 2, l * HQ + HQ - 1, 0)
                add(NQ - 1, l * HQ + HQ - 1, 1)
                for g in range(NG):
                    v.wait_ge(agg_tr, l * NG + g + 1)
                    V.tensor_copy(aggT[:, g * GT * P:(g + 1) * GT * P],
                                  grp_ps[g % 2][0:EH, 0:GT * P]).then_inc(aggT_ready, 1)
                with v.Fori(0, HCH) as c:
                    for s in range(2):
                        v.wait_ge(upd_ps[s], l * HCH + c + 1)
                        h_at = hT[:, bass.ds((2 * c + s) * CH, CH)]
                        V.scalar_tensor_tensor(h_at, psum[:, 6 + s, 0:CH], c2_sb[:, 0:1], h_at,
                                               ALU.add, ALU.add).then_inc(h_ready, 1)

            v.wait_ge(x_back, DMA * (2 if NB > 1 else 1))
            for g in range(NG):
                at = slice(g * GT, (g + 1) * GT)
                v.wait_ge(o_ps, g + 1)
                V.tensor_tensor(y[:, at, :], grp_ps[g % 2][:, 0:GT * F].rearrange("p (i f) -> p i f", f=F),
                                node_sb[:, at, :], ALU.add).then_inc(o_out, 1)
            v.wait_ge(o_out, NG)
            step(V.tensor_tensor(y[:, :, :], y[:, :, :], b_out_bc[:, :].unsqueeze(1).to_broadcast([P, NB, F]), ALU.add))
            step(V.reduce_sum(stat[:, 0, :], y[:, :, :], AX.X))
            step(V.tensor_scalar(stat[:, 0, :], stat[:, 0, :], 1.0 / F, None, ALU.mult))
            step(V.tensor_tensor(y[:, :, :], y[:, :, :], stat[:, 0, :].unsqueeze(2).to_broadcast([P, NB, F]), ALU.subtract))
            step(V.tensor_tensor(sq[:, :, :], y[:, :, :], y[:, :, :], ALU.mult))
            step(V.reduce_sum(stat[:, 1, :], sq[:, :, :], AX.X))
            V.tensor_scalar(stat[:, 1, :], stat[:, 1, :], 1.0 / F, 1e-5, ALU.mult, ALU.add).then_inc(fin_step, 1)
            v.wait_ge(sqrt_done, 1)
            step(V.reciprocal(stat[:, 3, :], stat[:, 2, :]))
            V.tensor_tensor(y[:, :, :], y[:, :, :], stat[:, 3, :].unsqueeze(2).to_broadcast([P, NB, F]),
                            ALU.mult).then_inc(o_ready, 1)

        @block.scalar
        def _(act):
            A = nc.scalar
            act.wait_ge(consts, N_CONSTS)
            for to, frm in ((src_raw, src), (dst_raw, dst)):
                if P > 1:
                    act.dma_start(to[0:P - 1, :], frm[0:(P - 1) * NC].rearrange("(p c) -> p c", c=NC)).then_inc(edges_in, DMA)
                act.dma_start(to[P - 1:P, 0:CTAIL], frm[(P - 1) * NC:E].rearrange("(p c) -> p c", p=1)).then_inc(edges_in, DMA)
            for g in range(NG):
                act.wait_ge(x_tr, g + 1)
                A.copy(xT[:, g * GT * P:(g + 1) * GT * P], grp_ps[g % 2][0:F, 0:GT * P]).then_inc(x_tr_out, 1)
            for c in range(NCH):
                act.wait_ge(h0_ps, c + 1)
                A.activation(hT[:, c * CH:(c + 1) * CH], psum[:, 4 + c % 2, 0:CH], ACT.Identity,
                             bias=b_in_sb[:, 0:1]).then_inc(h_ready, 1)
            act.wait_ge(sorted_, 1)
            with act.Fori(0, L) as l:
                for g in range(NG):
                    act.wait_ge(tab_ps, l * NG + g + 1)
                    ps = grp_ps[g % 2][:, 0:GT * P].rearrange("p (i c) -> p i c", c=P)
                    A.copy(src_table[:, g * GT:(g + 1) * GT, 0, :], ps[:, :, 0:EH]).then_inc(tab_hi, 1)
                act.wait_ge(tab_r, 3 * (l + 1) * NG)

                def prepare(q, it, s):
                    act.wait_ge(gathered[s], DMA * TPQ * it)
                    A.copy(idx_stage[:, s, :], dst_idx[:, bass.ds(q * TPQ, TPQ)]).then_inc(idx_ready[s], 1)
                    _, bucket = nc.values_load_multi_w_load_instructions(
                        pair_bucket[0:1, bass.ds(q * PPQ, PPQ)], engines=ACT_ONLY, min_val=0, max_val=NB - 1,
                        skip_runtime_bounds_check_because="a count of buckets that end before is 0 to NB - 1")
                    act.wait_ge(pre_ready[s], it)
                    for k in range(PPQ):
                        A.copy(src_rows[:, s, k, :, :],
                               src_table[:, bass.ds(bucket[k], 1), :, :].rearrange("p o k e -> p (o k) e"),
                               ).then_inc(rows_ready[s], 1)

                def silus(it, s):
                    act.wait_ge(pre_ready[s], it + 1)
                    act.wait_ge(z_ready[s], it)
                    A.activation(s1[:, s, :], pre_ps[:, s, :], ACT.Silu).then_inc(s1_ready[s], 1)
                    act.wait_ge(z_ready[s], it + 1)
                    act.wait_ge(agg_ready[s], it)
                    A.activation(msg[:, s, :, :].rearrange("p t e -> p (t e)"), z_ps[:, s, :],
                                 ACT.Silu).then_inc(msg_ready[s], 1)

                prepare(0, l * HQ, 0)
                if HQ > 1:
                    with act.Fori(0, HQ - 1) as j:
                        prepare(2 * j + 1, l * HQ + j, 1)
                        silus(l * HQ + j, 0)
                        prepare(2 * j + 2, l * HQ + j + 1, 0)
                        silus(l * HQ + j, 1)
                prepare(NQ - 1, l * HQ + HQ - 1, 1)
                silus(l * HQ + HQ - 1, 0)
                silus(l * HQ + HQ - 1, 1)
                with act.Fori(0, HCH) as c:
                    for s in range(2):
                        act.wait_ge(u_ps_ready[s], l * HCH + c + 1)
                        act.wait_ge(upd_ps[s], l * HCH + c)
                        A.activation(u_sb[:, s, :], psum[:, 4 + s, 0:CH], ACT.Silu,
                                     bias=c1_sb[:, 0:1]).then_inc(u_ready[s], 1)
            act.wait_ge(fin_step, 1)
            A.activation(stat[:, 2, :], stat[:, 1, :], ACT.Sqrt).then_inc(sqrt_done, 1)

        @block.tensor
        def _(pe):
            def mm(o, a, b, start=True, stop=True):
                return nc.tensor.matmul(o, a, b, start=start, stop=stop)

            pe.wait_ge(seq, 7)
            pe.wait_ge(loaded, DMA * N_LOADED)
            for g in range(NG):
                if g >= 2:
                    pe.wait_ge(x_tr_out, g - 1)
                for i in range(GT):
                    last = mm(grp_ps[g % 2][0:F, i * P:(i + 1) * P], node_sb[:, g * GT + i, :], ident[:, :])
                last.then_inc(x_tr, 1)
            pe.wait_ge(x_tr_out, NG)
            for c in range(NCH):
                if c >= 2:
                    pe.wait_ge(h_ready, c - 1)
                mm(psum[:, 4 + c % 2, 0:CH], W_in_sb[:, :], xT[:, c * CH:(c + 1) * CH]).then_inc(h0_ps, 1)
            pe.wait_ge(count_step, NB)
            mm(cnt_ps[:, 0:NB], tri[:, :], cnt[:, :]).then_inc(summed, 1)
            mm(cnt_ps[:, NB:2 * NB], ones[:, :], cnt[:, :]).then_inc(summed, 1)
            pe.wait_ge(recv_ready, 1)
            pe.wait_ge(h_ready, NCH)
            for k in range(NRB):
                last = mm(rt_ps[0:RB, k * P:(k + 1) * P], recv_b[:, k * RB:(k + 1) * RB], ident_b[:, :])
            last.then_inc(recv_tr, 1)
            pe.wait_ge(sorted_, 1)

            with pe.Fori(0, L) as l:
                pe.wait_ge(weights, DMA * N_WEIGHTS * (l + 1))
                pe.wait_ge(h_ready, (l + 1) * NCH)
                for g in range(NG):
                    if g >= 2:
                        pe.wait_ge(tab_done, l * NG + g - 1)
                        pe.wait_ge(tab_r, 3 * (l * NG + g - 2) + 1)
                    for i in range(GT):
                        n = g * GT + i
                        last = mm(grp_ps[g % 2][:, i * P:(i + 1) * P], hT[:, n * P:(n + 1) * P], w1_sb[:, :])
                    last.then_inc(tab_ps, 1)
                pe.wait_ge(tab_done, (l + 1) * NG)
                pe.wait_ge(tab_r, 3 * (l + 1) * NG)
                pe.wait_ge(b2_step, 8 * (l + 1))
                pe.sem_inc(turn, 1)
                with pe.Fori(0, HQ) as j:
                    for s in range(2):
                        it = l * HQ + j
                        pe.wait_ge(gathered[s], DMA * TPQ * (it + 1))
                        pe.wait_ge(s1_ready[s], it)
                        for k in range(PPQ):
                            mm(pre_ps[:, s, k * P:(k + 1) * P], gath[:, s, k * P:(k + 1) * P], ident[:, :],
                               start=k == 0, stop=False)
                        pe.wait_ge(pick_ready[s], it + 1)
                        pe.wait_ge(rows_ready[s], PPQ * (it + 1))
                        for k in range(PPQ):
                            for part3 in range(3):
                                for h in range(TPP):
                                    t = k * TPP + h
                                    last = mm(pre_ps[h * EH:(h + 1) * EH, s, k * P:(k + 1) * P],
                                              src_rows[:, s, k, part3, :], pick[:, s, t * P:(t + 1) * P],
                                              start=False, stop=k == PPQ - 1 and part3 == 2)
                        last.then_inc(pre_ready[s], 1)
                        pe.wait_ge(msg_ready[s], it)
                        mm(z_ps[:, s, :], ones_b[:, :], b2_parts[:, :, :].rearrange("p t e -> p (t e)"), stop=False)
                        pe.wait_ge(s1_ready[s], it + 1)
                        for k in range(PPQ):
                            last = mm(z_ps[:, s, k * P:(k + 1) * P], s1[:, s, k * P:(k + 1) * P], w2_sb[:, :],
                                      start=False, stop=k == PPQ - 1)
                        last.then_inc(z_ready[s], 1)
                        pe.wait_ge(added[s], PPQ * it)
                        pe.wait_ge(pick_t_ready[s], it + 1)
                        pe.wait_ge(msg_ready[s], it + 1)
                        for k in range(PPQ):
                            for h in range(TPP):
                                t = k * TPP + h
                                last = mm(agg_ps[:, s, k * EH:(k + 1) * EH], pick_t[:, s, t, :], msg[:, s, t, :],
                                          start=h == 0, stop=h == TPP - 1)
                        last.then_inc(agg_ready[s], 1)
                for s in range(2):
                    pe.wait_ge(added[s], PPQ * HQ * (l + 1))
                for g in range(NG):
                    if g >= 2:
                        pe.wait_ge(aggT_ready, l * NG + g - 1)
                    for i in range(GT):
                        last = mm(grp_ps[g % 2][0:EH, i * P:(i + 1) * P], agg[:, g * GT + i, :], ident[:, :])
                    last.then_inc(agg_tr, 1)
                pe.wait_ge(aggT_ready, (l + 1) * NG)
                pe.sem_inc(turn, 1)
                with pe.Fori(0, HCH) as c:
                    for s in range(2):
                        pe.wait_ge(u_ready[s], l * HCH + c)
                        at = bass.ds((2 * c + s) * CH, CH)
                        mm(psum[:, 4 + s, 0:CH], m1h_sb[:, :], hT[:, at], stop=False)
                        mm(psum[:, 4 + s, 0:CH], m1a_sb[:, :], aggT[:, at], start=False).then_inc(u_ps_ready[s], 1)
                    for s in range(2):
                        pe.wait_ge(u_ready[s], l * HCH + c + 1)
                        pe.wait_ge(h_ready, (l + 1) * NCH + 2 * c + s - 1)
                        mm(psum[:, 6 + s, 0:CH], m2_sb[:, :], u_sb[:, s, :]).then_inc(upd_ps[s], 1)
            pe.wait_ge(h_ready, (L + 1) * NCH)
            for g in range(NG):
                if g >= 2:
                    pe.wait_ge(o_out, g - 1)
                for i in range(GT):
                    n = g * GT + i
                    last = mm(grp_ps[g % 2][:, i * F:(i + 1) * F], hT[:, n * P:(n + 1) * P], W_out_sb[:, :])
                last.then_inc(o_ps, 1)


_INS = ['x', 'src', 'dst'] + ['L0_gnn_' + n for n in
                              ('W_in', 'b_in', 'eW1', 'eb1', 'eW2', 'eb2', 'nW1', 'nb1', 'nW2', 'nb2', 'W_out', 'b_out')]


def kernel(**inputs):
    import numpy as _np
    import concourse.bacc as _bacc
    from concourse import mybir as _mybir
    from concourse.bass_utils import run_bass_kernel_spmd as _run

    nc = _bacc.Bacc("TRN2", target_bir_lowering=False, num_devices=1)
    arrays, args = {}, []
    for name in _INS:
        a = _np.ascontiguousarray(inputs[name])
        arrays[f"in_{name}_dram"] = a
        args.append(nc.dram_tensor(f"in_{name}_dram", a.shape, _mybir.dt.from_np(a.dtype), kind="ExternalInput").ap())
    shape = tuple(arrays["in_x_dram"].shape)
    args.append(nc.dram_tensor("out_dram", shape, _mybir.dt.float32, kind="ExternalOutput").ap())
    build_gnn(nc, *args)
    r = _run(nc, [arrays], core_ids=[0])
    return r.results[0]["out_dram"]
```

```python
import concourse.bass as bass
from concourse import mybir
from contextlib import ExitStack

F32 = mybir.dt.float32
BF16 = mybir.dt.bfloat16
I32 = mybir.dt.int32
ALU = mybir.AluOpType
ACT = mybir.ActivationFunctionType
AX = mybir.AxisListType
DVE_ONLY = [mybir.EngineType.DVE]
ACT_ONLY = [mybir.EngineType.Activation]

P = 128
TPQ = 8
PPQ = TPQ // 2
DMA = 16
ROUND = 12582912.0


def done(n):
    return n + 1


def divisor(n, most, even_count=False):
    return max(d for d in range(1, most + 1) if n % d == 0 and not (even_count and (n // d) % 2))


def build_gnn(nc, x, src, dst, W_in, b_in, eW1, eb1, eW2, eb2, nW1, nb1, nW2, nb2, W_out, b_out, out):
    N, F = x.shape
    E = src.shape[0]
    H = W_in.shape[1]
    L, _, EH = eW1.shape
    assert H == P and EH * 2 == P and F == EH
    NT = divisor(N, P)
    NB = N // NT
    GT = divisor(NB, 5, even_count=True)
    NG = NB // GT
    NI = NB // 2
    NC = -(-E // P)
    CTAIL = E - (P - 1) * NC
    assert 0 < CTAIL <= NC and NC - CTAIL <= P
    SB = divisor(NC, 16, even_count=True)
    NBAT = NC // SB
    GPB = -(-SB // 2)
    CB = divisor(NC, P)
    MEAN = E / NB ** 2
    BT = -(-int((MEAN + MEAN ** 0.5) * NB) // P)
    BT += BT % 2
    C = BT * P // NB
    FASTT = NB * BT
    UNITS = [(u, min(TPQ, BT - u)) for u in range(0, BT, TPQ)]
    NU = len(UNITS)
    NQ = -(-((E + NB * (P - 1)) // P) // TPQ)
    NQ += NQ % 2
    T = NQ * TPQ
    TT = FASTT + 1 + T
    RBF, RBG = divisor(FASTT, P), divisor(T, P)

    def pieces(tiles, first):
        half = tiles // 2 * P
        found = ([], [])
        for h in range(2):
            q = at = first * P + h * half
            while q < at + half and q // C < NB:
                end = min(at + half, (q // C + 1) * C)
                found[h].append((h, q - at, end - q, q // C))
                q = end
        both = []
        for k in range(max(map(len, found))):
            both += [f[k] for f in found if k < len(f)]
        return both

    records = nc.dram_tensor("records", (P * TT, 2), I32).ap()
    cell_rows = nc.dram_tensor("cell_rows", (NC, P), F32).ap()
    dtile_rows = nc.dram_tensor("dtile_rows", (NC, P), BF16).ap()
    src_rows_d = nc.dram_tensor("src_rows_d", (FASTT, P), BF16).ap()
    dst_rows_d = nc.dram_tensor("dst_rows_d", (FASTT, P), BF16).ap()
    gen_rows_d = nc.dram_tensor("gen_rows_d", (T, P), BF16).ap()
    dst_table = nc.dram_tensor("dst_table", (N, EH), F32).ap()

    with ExitStack() as ctx:
        def sb(name, shape, dt, c=ctx):
            return c.enter_context(nc.sbuf_tensor(name, shape, dt))

        def sem(name, n=0):
            if n:
                return [ctx.enter_context(nc.semaphore(f"{name}{k}")) for k in range(n)]
            return ctx.enter_context(nc.semaphore(name))

        ident = sb("ident", [P, P], F32)
        ident_b = sb("ident_b", [P, P], BF16)
        ones_b = sb("ones_b", [P, P], BF16)
        zeros_b = sb("zeros_b", [P, P], BF16)
        part = sb("part", [P, 1], F32)
        lane = sb("lane", [P, P], F32)
        pick3 = sb("pick3", [P, 3], F32)

        W_in_sb = sb("W_in_sb", [F, H], F32)
        b_in_sb = sb("b_in_sb", [H, 1], F32)
        w1_sb = sb("w1_sb", [H, P], F32)
        b1_bc = sb("b1_bc", [P, P], F32)
        w2_sb = sb("w2_sb", [P, P], F32)
        b2_bc = sb("b2_bc", [P, EH], F32)
        b2_hi = sb("b2_hi", [P, EH], BF16)
        b2_mid = sb("b2_mid", [P, EH], BF16)
        b2_r1 = sb("b2_r1", [P, EH], F32)
        b2_r2 = sb("b2_r2", [P, EH], F32)
        b2_sum = sb("b2_sum", [P, EH], F32)
        b2_parts = sb("b2_parts", [P, TPQ, EH], BF16)
        m1h_sb = sb("m1h_sb", [H, H], F32)
        m1a_sb = sb("m1a_sb", [EH, H], F32)
        c1_sb = sb("c1_sb", [H, 1], F32)
        m2_sb = sb("m2_sb", [H, H], F32)
        c2_sb = sb("c2_sb", [H, 1], F32)
        W_out_sb = sb("W_out_sb", [H, F], F32)
        b_out_bc = sb("b_out_bc", [P, F], F32)

        hT = sb("hT", [H, N], F32)
        recv = sb("recv", [P, FASTT], BF16)
        g_recv = sb("g_recv", [P, T], BF16)
        g_dst = sb("g_dst", [P, T], I32)
        tile_bucket = sb("tile_bucket", [P, T], I32)
        trips = sb("trips", [P, 1], I32)

        with ExitStack() as early:
            tri = sb("tri", [P, P], F32, early)
            ones = sb("ones", [P, P], F32, early)
            before = sb("before", [P, 2, 2 * P], F32, early)
            tile_i = sb("tile_i", [P, NB], F32, early)
            col_no = sb("col_no", [P, NC], F32, early)
            x_sb = sb("x_sb", [P, NB, F], F32, early)
            xT = sb("xT", [F, 2, GT * NT], F32, early)
            src_raw = sb("src_raw", [P, NC], I32, early)
            dst_raw = sb("dst_raw", [P, NC], I32, early)
            stile = sb("stile", [P, NC], BF16, early)
            dtile = sb("dtile", [P, NC], BF16, early)
            cell = sb("cell", [P, NC], F32, early)
            base = sb("base", [P, NC], F32, early)
            tmp1 = sb("tmp1", [P, NC], F32, early)
            tmp2 = sb("tmp2", [P, NC], F32, early)
            cell_t = sb("cell_t", [CB, NC // CB, P], F32, early)
            dtile_t = sb("dtile_t", [CB, NC // CB, P], BF16, early)
            cell_bc = sb("cell_bc", [P, 2, SB * P], F32, early)
            dtile_bc = sb("dtile_bc", [NB, 2, SB * P], BF16, early)
            oh_d = sb("oh_d", [NB, 2, SB * P], F32, early)
            oh_dt = sb("oh_dt", [P, 2, SB, NB], BF16, early)
            oh_st = sb("oh_st", [P, 2, SB, NB], BF16, early)
            look = sb("look", [NB, 2, 2, NB], F32, early)
            prod = sb("prod", [P, 2, 2, 2, NB], F32, early)
            eq = sb("eq", [P, 2, 2 * P], F32, early)
            r_cell = sb("r_cell", [P, 2, 2 * GPB, 2], F32, early)
            r_in = sb("r_in", [P, 2, SB], F32, early)
            f_d = sb("f_d", [P, SB], F32, early)
            f_r = sb("f_r", [P, SB], F32, early)
            f_t = sb("f_t", [P, SB], F32, early)
            f_u = sb("f_u", [P, SB], F32, early)
            f_lin = sb("f_lin", [P, SB], I32, early)
            f_lo = sb("f_lo", [P, SB], I32, early)
            f_hi = sb("f_hi", [P, SB], I32, early)
            pos_stage = sb("pos_stage", [P, 2, SB], I32, early)
            rec_stage = sb("rec_stage", [P, 2, SB, 2], I32, early)
            excess = sb("excess", [NB, NB], F32, early)
            tot_i = sb("tot_i", [P, NB], I32, early)
            ntile_i = sb("ntile_i", [P, NB], I32, early)
            ntile = sb("ntile", [P, NB], F32, early)
            tile_end = sb("tile_end", [P, NB], F32, early)
            first = sb("first", [P, NB], F32, early)
            trips_i = sb("trips_i", [P, 2], I32, early)
            PADT = 512
            pads = sb("pads", [P, PADT, 2], I32, early)
            tile_f = sb("tile_f", [P, T], F32, early)
            tile_no = sb("tile_no", [P, T], F32, early)
        with ExitStack() as mid:
            recs = sb("recs", [P, max(FASTT, T), 2], I32, mid)
            rf = sb("rf", [P, FASTT], F32, mid)
            rt = sb("rt", [P, FASTT], F32, mid)
            rb = sb("rb", [P, FASTT], BF16, mid)
            rows_t = sb("rows_t", [P, 2048], BF16, mid)

        aggT = sb("aggT", [P, max(N, 2 * NB * F)], F32)
        x_fin = aggT[:, 0:NB * F].rearrange("p (i f) -> p i f", f=F)
        sq = aggT[:, NB * F:2 * NB * F].rearrange("p (i f) -> p i f", f=F)
        agg = sb("agg", [P, NB, EH], F32)
        y = agg
        table = sb("table", [P, NB + 2, 3, P], BF16)
        tab_f = sb("tab_f", [P, 2, GT, P], F32)
        tab_r1 = sb("tab_r1", [P, 2, GT, P], F32)
        ids_bc = sb("ids_bc", [P, 2, 2, TPQ * P], BF16)
        pick = sb("pick", [P, 2, 2, TPQ * P], BF16)
        pick_g = sb("pick_g", [P, 2, TPQ, P], F32)
        pick_t = pick_g[:, :, 0:TPQ // 2, :].rearrange("p s t n -> p s (t n)").bitcast(BF16).rearrange(
            "p s (t n) -> p s t n", n=P)
        rows = sb("rows", [P, 2, 3, EH], BF16)
        rows_g = sb("rows_g", [P, 2, TPQ, 3, EH], BF16)
        idx_stage = sb("idx_stage", [P, 2, TPQ], I32)
        gath = sb("gath", [P, 2, TPQ * EH], F32)
        s1 = sb("s1", [P, 2, PPQ * P], F32)
        msg = sb("msg", [P, 2, TPQ, EH], F32)
        msg_r1 = sb("msg_r1", [P, 2, TPQ, EH], F32)
        msg3 = sb("msg3", [P, 2, TPQ, 3, EH], BF16)
        u_sb = sb("u_sb", [H, 2, NT], F32)
        stat = sb("stat", [P, 4, NB], F32)

        psum = ctx.enter_context(nc.psum_tensor("psum", [P, 8, 512], F32))

        def bank2(k):
            return psum[:, k:k + 2, :].rearrange("p b c -> p (b c)")

        pre_ps = psum[:, 0:2, :]
        z_ps = psum[:, 2:4, :]
        agg_ps = psum[:, 4:6, :]
        grp_ps = [bank2(0), bank2(2)]
        xt_ps = [bank2(4), bank2(6)]
        t_ps = psum[:, 4:8, :].rearrange("p b c -> p (b c)")
        cnt_ps = psum[0:NB, 0, 0:NB]
        look_ps = psum[:, 1:3, :]
        group_ps = [psum[0:NB, 4 + k, 0:NB] for k in range(2)]
        exc_ps = psum[:, 3, :]

        loaded, edges_in, consts = sem("loaded"), sem("edges_in"), sem("consts")
        turn = sem("turn")
        padded, pad_set = sem("padded"), sem("pad_set")
        seq = sem("seq")
        x_tr, x_tr_out, h0_ps, h_ready = sem("x_tr"), sem("x_tr_out"), sem("h0_ps"), sem("h_ready")
        t_ready = sem("t_ready")
        t_done = sem("t_done")
        t_copied = sem("t_copied")
        t_out = sem("t_out")
        cells_out = sem("cells_out")
        c_oh = sem("c_oh", 2)
        c_used = sem("c_used", 2)
        counted = sem("counted")
        excess_ready, summed, look_ready = sem("excess_ready"), sem("summed"), sem("look_ready")
        bc_in = sem("bc_in", 2)
        oh_ready = sem("oh_ready", 2)
        batch_done = sem("batch_done", 2)
        looked = sem("looked")
        grouped = sem("grouped")
        count_set = sem("count_set")
        look_read = sem("look_read")
        rk = sem("rk")
        staged = sem("staged", 2)
        scattered = sem("scattered", 2)
        recs_in = sem("recs_in")
        sorted_ = sem("sorted")
        tile_step = sem("tile_step")
        weights, b2_step, b1_zero = sem("weights"), sem("b2_step"), sem("b1_zero")
        tab_ps, tab_sum, tab_hi, tab_r, tab_mid, tab_done = (sem(n) for n in
            ("tab_ps", "tab_sum", "tab_hi", "tab_r", "tab_mid", "tab_done"))
        table_out = sem("table_out", 2)
        ids_in, pick_ready, pick_t_ready = sem("ids_in", 2), sem("pick_ready", 2), sem("pick_t_ready", 2)
        rows_ready, pre_ready, s1_ready, z_ready = (sem(n, 2) for n in ("rows_ready", "pre_ready", "s1_ready", "z_ready"))
        hi_ready, msg3_ready, agg_ready = sem("hi_ready", 2), sem("msg3_ready", 2), sem("agg_ready", 2)
        msg_set = sem("msg_set")
        bucket_out = sem("bucket_out", 2)
        r1_ready, mid_ready = sem("r1_ready", 2), sem("mid_ready", 2)
        g_ids_in, g_pick_ready, g_pick_t_ready = sem("g_ids_in", 2), sem("g_pick_ready", 2), sem("g_pick_t_ready", 2)
        g_rows_ready, g_idx_ready, gathered = sem("g_rows_ready", 2), sem("g_idx_ready", 2), sem("gathered", 2)
        g_pre_ready, g_s1_ready, g_z_ready = (sem(n, 2) for n in ("g_pre_ready", "g_s1_ready", "g_z_ready"))
        g_msg_ready, g_agg_ready, g_added = (sem(n, 2) for n in ("g_msg_ready", "g_agg_ready", "g_added"))
        agg_tr, aggT_ready = sem("agg_tr"), sem("aggT_ready")
        u_ps_ready, u_ready, upd_ps = sem("u_ps_ready", 2), sem("u_ready", 2), sem("upd_ps", 2)
        x_back, o_ps, o_out, o_ready, fin_step, sqrt_done, stored = (sem(n) for n in
            ("x_back", "o_ps", "o_out", "o_ready", "fin_step", "sqrt_done", "stored"))

        N_WEIGHTS = 11
        N_CONSTS = 7
        SU = NI * NU

        block = ctx.enter_context(nc.Block())

        def unit(i, n):
            return (i, n) if n >= 0 else (i - 1, n + 2 * NU)

        def over_units(eng, step, lag):
            for n in range(2 * NU):
                step(0, n, first=True)
            if NI > 1:
                with eng.Fori(1, NI) as i:
                    for n in range(2 * NU):
                        step(i, n)
            for n in range(lag):
                step(NI, n, last=True)

        def bc(ap, shape, *dims):
            for d in dims:
                ap = ap.unsqueeze(d)
            return ap.to_broadcast(shape)

        @block.sync
        def _(sp):
            x_v = x.rearrange("(i p) f -> p i f", p=NT)
            sp.dma_start(x_sb[0:NT, :, :], x_v).then_inc(loaded, DMA)
            sp.dma_start(W_in_sb[:, :], W_in).then_inc(loaded, DMA)
            sp.dma_start(b_in_sb[:, :], b_in.rearrange("(h o) -> h o", o=1)).then_inc(loaded, DMA)
            sp.dma_start(W_out_sb[:, :], W_out).then_inc(loaded, DMA)
            sp.dma_start(b_out_bc[:, :], b_out.partition_broadcast(P)).then_inc(loaded, DMA)
            sp.wait_ge(pad_set, 2)
            records_v = records.rearrange("(p t) c -> p t c", p=P)
            for t in range(0, TT, PADT):
                n = min(PADT, TT - t)
                sp.dma_start(records_v[:, t:t + n, :], pads[:, 0:n, :]).then_inc(padded, DMA)
            sp.wait_ge(t_copied, 1)
            sp.dma_start(cell_rows.rearrange("(b r) p -> r b p", r=CB), cell_t[:, :, :]).then_inc(cells_out, DMA)
            sp.wait_ge(t_copied, 2)
            sp.dma_start(dtile_rows.rearrange("(b r) p -> r b p", r=CB), dtile_t[:, :, :]).then_inc(cells_out, DMA)
            sp.wait_ge(cells_out, 2 * DMA)
            with sp.Fori(0, NBAT // 2) as j:
                for s in range(2):
                    at = bass.ds((2 * j + s) * SB, SB)
                    sp.wait_ge(batch_done[s], done(j))
                    sp.dma_start(cell_bc[:, s, :], cell_rows[at, :].rearrange("t p -> (t p)").partition_broadcast(P)).then_inc(bc_in[s], DMA)
                    sp.dma_start(dtile_bc[:, s, :], dtile_rows[at, :].rearrange("t p -> (t p)").partition_broadcast(NB)).then_inc(bc_in[s], DMA)
            for s in range(2):
                sp.wait_ge(scattered[s], DMA * (NC // 2))
            sp.wait_ge(sorted_, 1)
            sp.dma_start(recs[:, 0:FASTT, :], records_v[:, 0:FASTT, :]).then_inc(recs_in, DMA)
            for k, (d, r) in enumerate(((src_rows_d, RBF), (dst_rows_d, RBF), (gen_rows_d, RBG))):
                sp.wait_ge(t_copied, 3 + k)
                n = d.shape[0] // r
                sp.dma_start(d.rearrange("(b r) p -> r b p", r=r),
                             rows_t[0:r, 0:n * P].rearrange("r (b p) -> r b p", p=P)).then_inc(t_out, DMA)
                if k == 0:
                    sp.wait_ge(sorted_, 2)
                    sp.dma_start(recs[:, 0:T, :], records_v[:, FASTT + 1:TT, :]).then_inc(recs_in, DMA)
            sp.wait_ge(t_out, 3 * DMA)
            more = sp.value_load(trips[0:1, 0:1], min_val=1, max_val=NQ // 2 - 1)
            n_trips = more + 1
            with sp.Fori(0, L) as l:
                sp.wait_ge(h_ready, (l + 1) * NB)
                sp.wait_ge(sorted_, 4)
                dl = bass.ds(l, 1)
                for to, frm in ((w1_sb[:, 0:EH], eW1[dl, 0:H, :]), (w1_sb[:, EH:P], eW1[dl, H:2 * H, :]),
                                (w2_sb[0:EH, 0:EH], eW2[dl, :, :]), (w2_sb[EH:P, EH:P], eW2[dl, :, :]),
                                (m1h_sb[:, :], nW1[dl, 0:H, :]), (m1a_sb[:, :], nW1[dl, H:H + EH, :]),
                                (m2_sb[:, :], nW2[dl, :, :])):
                    sp.dma_start(to, frm.rearrange("o h e -> (o h) e")).then_inc(weights, DMA)
                for to, frm in ((b1_bc[:, EH:P], eb1), (b2_bc[:, :], eb2)):
                    sp.dma_start(to, frm[dl, :].rearrange("o e -> (o e)").partition_broadcast(P)).then_inc(weights, DMA)
                sp.dma_start(c1_sb[:, :], nb1[dl, :].rearrange("o h -> h o")).then_inc(weights, DMA)
                sp.dma_start(c2_sb[:, :], nb2[dl, :].rearrange("o h -> h o")).then_inc(weights, DMA)

                def ids(i, n, first=False, last=False):
                    b, (u, tiles) = n // NU, UNITS[n % NU]
                    s, cnt = n % 2, l * SU + i * NU + n // 2
                    sp.wait_ge(pick_ready[s], done(2 * cnt))
                    for k, d in enumerate((src_rows_d, dst_rows_d)):
                        sp.dma_start(ids_bc[:, s, k, 0:tiles * P],
                                     d[bass.ds((2 * i + b) * BT + u, tiles), :].rearrange("t p -> (t p)")
                                     .partition_broadcast(P)).then_inc(ids_in[s], DMA)

                for n in range(2):
                    ids(0, n)
                for g in range(NG):
                    sp.wait_ge(tab_sum, l * NG + g + 1)
                    sp.dma_start(dst_table[g * GT * NT:(g + 1) * GT * NT, :].rearrange("(i p) e -> p i e", p=NT),
                                 tab_f[0:NT, g % 2, :, EH:P]).then_inc(table_out[g % 2], DMA)
                for n in range(2, 2 * NU):
                    ids(0, n)
                if NI > 1:
                    with sp.Fori(1, NI) as i:
                        for n in range(2 * NU):
                            ids(i, n)
                for s in range(2):
                    sp.wait_ge(pick_ready[s], done(2 * (l + 1) * SU))
                    sp.sem_inc(turn, 1)
                with sp.Fori(0, n_trips) as j:
                    for s in range(2):
                        it = l * n_trips + j
                        sp.wait_ge(g_pick_ready[s], done(it))
                        sp.dma_start(ids_bc[:, s, 0, :], gen_rows_d[bass.ds((2 * j + s) * TPQ, TPQ), :]
                                     .rearrange("t p -> (t p)").partition_broadcast(P)).then_inc(g_ids_in[s], DMA)
                for s in range(2):
                    sp.wait_ge(g_pick_ready[s], done((l + 1) * n_trips))
                    sp.sem_inc(turn, 1)
            sp.wait_ge(h_ready, (L + 1) * NB)
            sp.dma_start(x_fin[0:NT, :, :], x_v).then_inc(x_back, DMA)
            sp.wait_ge(o_ready, 1)
            sp.dma_start(out.rearrange("(i p) f -> p i f", p=NT), y[0:NT, :, :]).then_inc(stored, DMA)
            sp.wait_ge(stored, DMA)

        @block.gpsimd
        def _(pool):
            G = nc.gpsimd
            for to, pattern, b0, mult in ((lane, [[1, P]], 0, 0), (part, [[1, 1]], 0, 1), (tile_i, [[1, NB]], 0, 0),
                                          (col_no, [[1, NC]], P - NC, 0), (tile_no, [[1, T]], 0, 0)):
                G.iota(to[:, :], pattern, base=b0, channel_multiplier=mult,
                       allow_small_or_imprecise_dtypes=True).then_inc(consts, 1)
            G.memset(src_raw[:, :], N).then_inc(consts, 1)
            G.memset(dst_raw[:, :], 0).then_inc(consts, 1)
            G.memset(pads[:, :, 0], -1).then_inc(pad_set, 1)
            G.memset(pads[:, :, 1], 0).then_inc(pad_set, 1)
            pool.wait_ge(padded, DMA * -(-TT // PADT))
            with pool.Fori(0, NBAT // 2) as j:
                for s in range(2):
                    pool.wait_ge(staged[s], 3 * (j + 1))
                    pool.sem_inc(turn, 1)
                    for c in range(SB):
                        G.indirect_dma_start(
                            out=records, out_offset=bass.IndirectOffsetOnAxis(ap=pos_stage[:, s, c:c + 1], axis=0),
                            in_=rec_stage[:, s, c, :], in_offset=None).then_inc(scattered[s], DMA)
            pool.wait_ge(sorted_, 4)
            more = pool.value_load(trips[0:1, 0:1], min_val=1, max_val=NQ // 2 - 1)
            n_trips = more + 1
            with pool.Fori(0, L) as l:
                def gather(it, s):
                    pool.wait_ge(g_idx_ready[s], it + 1)
                    pool.sem_inc(turn, 1)
                    for t in range(TPQ):
                        G.indirect_dma_start(
                            out=gath[:, s, t * EH:(t + 1) * EH], out_offset=None, in_=dst_table,
                            in_offset=bass.IndirectOffsetOnAxis(ap=idx_stage[:, s, t:t + 1], axis=0),
                        ).then_inc(gathered[s], DMA)

                def cells(i, n, first=False):
                    tiles, s, cnt = UNITS[n % NU][1], n % 2, l * SU + i * NU + n // 2
                    pool.wait_ge(hi_ready[s], cnt + 1)
                    G.tensor_tensor(msg_r1[:, s, 0:tiles, :], msg[:, s, 0:tiles, :], msg3[:, s, 0:tiles, 0, :],
                                    ALU.subtract).then_inc(r1_ready[s], 1)
                    pool.wait_ge(mid_ready[s], cnt + 1)
                    G.tensor_tensor(msg3[:, s, 0:tiles, 2, :], msg_r1[:, s, 0:tiles, :], msg3[:, s, 0:tiles, 1, :],
                                    ALU.subtract).then_inc(msg3_ready[s], 1)

                for s in range(2):
                    gather(l * n_trips, s)
                over_units(pool, cells, 0)
                with pool.Fori(1, n_trips) as j:
                    for s in range(2):
                        gather(l * n_trips + j, s)

        @block.vector
        def _(v):
            V = nc.vector
            for s_ in (*pick_ready, *g_pick_ready, *g_added, *bucket_out, *batch_done, rk, tile_step, look_read, count_set):
                v.sem_inc(s_, done(0))
            n_seq = [0]

            def step(ins):
                n_seq[0] += 1
                ins.then_inc(seq, 1)
                v.wait_ge(seq, n_seq[0])

            v.wait_ge(consts, N_CONSTS)
            step(V.tensor_scalar(ident[:, :], lane[:, :], part[:, 0:1], None, ALU.is_equal))
            step(V.tensor_copy(ident_b[:, :], ident[:, :]))
            step(V.tensor_scalar(tri[:, :], lane[:, :], part[:, 0:1], None, ALU.is_gt))
            step(V.memset(ones[:, :], 1.0))
            step(V.memset(ones_b[:, :], 1.0))
            step(V.memset(zeros_b[:, :], 0.0))
            step(V.tensor_scalar(pick3[:, :], lane[:, 0:3], part[:, 0:1], None, ALU.is_equal))
            step(V.memset(w2_sb[:, :], 0.0))
            step(V.memset(b1_bc[:, :], 0.0))
            step(V.memset(before[:, :, :], 0.0))
            step(V.memset(look[:, :, :, :], 0.0))
            step(V.tensor_scalar(before[:, 0, 0:P], lane[:, :], part[:, 0:1], None, ALU.is_lt))
            step(V.memset(before[:, 1, 0:P], 1.0))
            step(V.tensor_scalar(before[:, 1, P:2 * P], lane[:, :], part[:, 0:1], None, ALU.is_lt))

            def tile_of(to, f, tmp, size=NT):
                step(V.tensor_scalar(tmp, f, 1.0 / size, -(size - 1) / (2.0 * size), ALU.mult, ALU.add))
                step(V.tensor_scalar(to, tmp, ROUND, -ROUND, ALU.add, ALU.add))

            v.wait_ge(edges_in, DMA * 4)
            step(V.tensor_copy(tmp1[:, :], src_raw[:, :]))
            tile_of(stile[:, :], tmp1[:, :], tmp2[:, :])
            step(V.scalar_tensor_tensor(src_raw[:, :], stile[:, :], -float(NT), tmp1[:, :], ALU.mult, ALU.add))
            step(V.tensor_copy(tmp1[:, :], dst_raw[:, :]))
            tile_of(dtile[:, :], tmp1[:, :], tmp2[:, :])
            step(V.scalar_tensor_tensor(tmp2[:, :], stile[:, :], float(NB), col_no[:, :], ALU.is_equal, ALU.mult))
            step(V.scalar_tensor_tensor(cell[:, :], stile[:, :], float(NB), dtile[:, :], ALU.mult, ALU.add))
            step(V.tensor_tensor(cell[:, :], cell[:, :], tmp2[:, :], ALU.add))
            v.sem_inc(t_ready, 2)
            step(V.scalar_tensor_tensor(base[:, :], stile[:, :], float(BT * P), tmp2[:, :], ALU.mult, ALU.add))
            step(V.scalar_tensor_tensor(base[:, :], dtile[:, :], float(C), base[:, :], ALU.mult, ALU.add))
            for k, (t, r) in enumerate(((cell_t, NC // CB), (dtile_t, NC // CB))):
                v.wait_ge(t_done, k + 1)
                V.tensor_copy(t[:, :, :].rearrange("r b p -> r (b p)"), t_ps[0:CB, 0:r * P]).then_inc(t_copied, 1)

            def one_hots(s, at, sems):
                for oh, t in ((oh_dt, dtile), (oh_st, stile)):
                    V.tensor_tensor(oh[:, s, :, :], bc(tile_i[:, :], [P, SB, NB], 1),
                                    bc(t[:, at], [P, SB, NB], 2), ALU.is_equal).then_inc(sems[s], 1)

            with v.Fori(0, NBAT // 2) as j:
                for s in range(2):
                    v.wait_ge(c_used[s], done(j))
                    one_hots(s, bass.ds((2 * j + s) * SB, SB), c_oh)
            v.wait_ge(counted, 1)
            V.tensor_scalar(excess[:, :], cnt_ps, -float(C), 0.0, ALU.add, ALU.max).then_inc(excess_ready, 1)
            v.wait_ge(summed, 2)
            step(V.tensor_scalar(tot_i[:, :], exc_ps[:, 0:NB], float(P - 1), None, ALU.add))
            step(V.tensor_scalar(ntile_i[:, :], tot_i[:, :], 7, None, ALU.logical_shift_right))
            step(V.tensor_copy(ntile[:, :], ntile_i[:, :]))
            step(V.tensor_tensor_scan(tile_end[:, :], ones[:, 0:NB], ntile[:, :], 0.0, ALU.mult, ALU.add))
            step(V.tensor_tensor(first[:, :], tile_end[:, :], ntile[:, :], ALU.subtract))
            step(V.tensor_scalar(first[:, :], first[:, :], float(P), float((FASTT + 1) * P - C), ALU.mult, ALU.add))
            for s in range(2):
                step(V.tensor_tensor(look[:, s, 1, :], exc_ps[0:NB, P:P + NB], first[0:NB, :], ALU.add))
            v.sem_inc(look_ready, 1)
            step(V.tensor_scalar(trips_i[:, 0:1], tile_end[:, NB - 1:NB], float(2 * TPQ - 1), None, ALU.add))
            step(V.tensor_scalar(trips_i[:, 1:2], trips_i[:, 0:1], 4, None, ALU.logical_shift_right))
            step(V.tensor_scalar(trips[:, :], trips_i[:, 1:2], 2.0, -1.0, ALU.max, ALU.add))
            step(V.memset(tile_f[:, :], 0.0))
            with v.Fori(0, NB - 1) as b:
                v.wait_ge(tile_step, done(b))
                V.scalar_tensor_tensor(tile_f[:, :], tile_no[:, :], tile_end[:, bass.ds(b, 1)], tile_f[:, :],
                                       ALU.is_ge, ALU.add).then_inc(tile_step, 1)
            v.wait_ge(tile_step, done(NB - 1))
            step(V.tensor_copy(tile_bucket[:, :], tile_f[:, :]))

            RK = GPB + 6

            def batch(j, s, first_time=False):
                n_rk = (2 * j + s) * RK
                at = bass.ds((2 * j + s) * SB, SB)
                one_hots(s, at, oh_ready)
                v.wait_ge(bc_in[s], 2 * DMA * (j + 1))
                V.tensor_scalar(oh_d[:, s, :], dtile_bc[:, s, :], part[0:NB, 0:1], None,
                                ALU.is_equal).then_inc(oh_ready[s], 1)
                for g in range(GPB):
                    c0 = 2 * g
                    k = min(2, SB - c0)
                    gs = (s * GPB + g) % 2
                    n = (2 * j + s) * GPB + g
                    v.wait_ge(grouped, n + 1)
                    v.wait_ge(count_set, done(n))
                    V.tensor_tensor(look[:, 1 - gs, 0, :], look[:, gs, 0, :], group_ps[gs], ALU.add).then_inc(count_set, 1)
                    for m in range(k):
                        V.scalar_tensor_tensor(eq[:, m, 0:(m + 1) * P], cell_bc[:, s, c0 * P:(c0 + m + 1) * P],
                                               cell[:, bass.ds((2 * j + s) * SB + c0 + m, 1)], before[:, m, 0:(m + 1) * P],
                                               ALU.is_equal, ALU.mult, accum_out=r_in[:, s, c0 + m:c0 + m + 1])
                    v.wait_ge(looked, n + 1)
                    V.tensor_tensor(prod[:, gs, 0:k, :, :],
                                    look_ps[:, gs, 0:k * 2 * NB].rearrange("p (c w i) -> p c w i", w=2, i=NB),
                                    bc(oh_st[:, s, c0:c0 + k, :], [P, k, 2, NB], 2), ALU.mult).then_inc(look_read, 1)
                    v.wait_ge(look_read, done(n + 1))
                    V.reduce_sum(r_cell[:, s, c0:c0 + k, :], prod[:, gs, 0:k, :, :], AX.X).then_inc(rk, 1)
                v.wait_ge(rk, done(n_rk + GPB))
                base_at = r_cell[:, s, 0:SB, 1]
                V.tensor_tensor(f_d[:, :], base[:, at], base_at, ALU.subtract)
                V.tensor_tensor(f_r[:, :], r_cell[:, s, 0:SB, 0], r_in[:, s, :], ALU.add).then_inc(rk, 1)
                v.wait_ge(rk, done(n_rk + GPB + 1))
                V.scalar_tensor_tensor(f_t[:, :], f_r[:, :], float(C), f_d[:, :], ALU.is_lt, ALU.mult)
                V.tensor_tensor(f_u[:, :], f_r[:, :], base_at, ALU.add).then_inc(rk, 1)
                v.wait_ge(rk, done(n_rk + GPB + 2))
                V.tensor_tensor(f_lin[:, :], f_t[:, :], f_u[:, :], ALU.add).then_inc(rk, 1)
                v.wait_ge(rk, done(n_rk + GPB + 3))
                V.tensor_scalar(f_lo[:, :], f_lin[:, :], P - 1, None, ALU.bitwise_and).then_inc(rk, 1)
                V.tensor_scalar(f_hi[:, :], f_lin[:, :], 7, None, ALU.logical_shift_right).then_inc(rk, 1)
                v.wait_ge(rk, done(n_rk + GPB + 5))
                if not first_time:
                    v.wait_ge(scattered[s], DMA * SB * j)
                V.scalar_tensor_tensor(pos_stage[:, s, :], f_lo[:, :], float(TT), f_hi[:, :],
                                       ALU.mult, ALU.add).then_inc(staged[s], 1)
                V.tensor_copy(f_d[:, 0:1], f_d[:, 0:1]).then_inc(rk, 1)
                v.wait_ge(rk, done(n_rk + RK))
                v.sem_inc(batch_done[s], 1)

            for s in range(2):
                batch(0, s, first_time=True)
            with v.Fori(1, NBAT // 2) as j:
                for s in range(2):
                    batch(j, s)
            for s in range(2):
                v.wait_ge(scattered[s], DMA * (NC // 2))
            v.sem_inc(sorted_, 1)

            v.wait_ge(recs_in, DMA)

            def transposed(k, r, n):
                v.wait_ge(t_done, k)
                if k > 3:
                    v.wait_ge(t_out, DMA * (k - 3))
                V.tensor_copy(rows_t[0:r, 0:n * P], t_ps[0:r, 0:n * P]).then_inc(t_copied, 1)

            step(V.tensor_copy(recv[:, :], recs[:, 0:FASTT, 0]))
            v.sem_inc(t_ready, 1)
            step(V.tensor_copy(rf[:, :], recs[:, 0:FASTT, 1]))
            v.sem_inc(sorted_, 1)
            tile_of(rt[:, :], rf[:, :], rt[:, :])
            step(V.scalar_tensor_tensor(rb[:, :], rt[:, :], -float(NT), rf[:, :], ALU.mult, ALU.add))
            transposed(3, RBF, FASTT // RBF)
            v.sem_inc(t_ready, 1)
            v.wait_ge(recs_in, 2 * DMA)
            step(V.tensor_copy(g_recv[:, :], recs[:, 0:T, 0]))
            step(V.tensor_copy(g_dst[:, :], recs[:, 0:T, 1]))
            transposed(4, RBF, FASTT // RBF)
            v.sem_inc(t_ready, 1)
            transposed(5, RBG, T // RBG)
            v.wait_ge(t_out, 3 * DMA)
            v.sem_inc(sorted_, 2)

            step(V.memset(table[:, NB:NB + 2, :, :], 0.0))
            with v.Fori(0, L) as l:
                v.wait_ge(weights, DMA * N_WEIGHTS * (l + 1))
                B2 = 8

                def b2(k, ins):
                    ins.then_inc(b2_step, 1)
                    v.wait_ge(b2_step, l * B2 + k)

                b2(1, V.tensor_copy(b2_hi[:, :], b2_bc[:, :]))
                b2(2, V.tensor_tensor(b2_r1[:, :], b2_bc[:, :], b2_hi[:, :], ALU.subtract))
                b2(3, V.tensor_copy(b2_mid[:, :], b2_r1[:, :]))
                b2(4, V.tensor_tensor(b2_r2[:, :], b2_r1[:, :], b2_mid[:, :], ALU.subtract))
                b2(5, V.tensor_scalar(b2_sum[:, :], b2_hi[:, :], pick3[:, 0:1], None, ALU.mult))
                b2(6, V.scalar_tensor_tensor(b2_sum[:, :], b2_mid[:, :], pick3[:, 1:2], b2_sum[:, :], ALU.mult, ALU.add))
                b2(7, V.scalar_tensor_tensor(b2_sum[:, :], b2_r2[:, :], pick3[:, 2:3], b2_sum[:, :], ALU.mult, ALU.add))
                b2(8, V.tensor_copy(b2_parts[:, :, :], bc(b2_sum[:, :], [P, TPQ, EH], 1)))
                for g in range(NG + 2):
                    if g < NG:
                        s, n = g % 2, l * NG + g
                        v.wait_ge(tab_ps, n + 1)
                        if g >= 2:
                            v.wait_ge(table_out[s], DMA * (l * (NG // 2) + g // 2))
                            v.wait_ge(tab_r, n - 1)
                        V.tensor_tensor(tab_f[0:NT, s, :, :], grp_ps[s][0:NT, 0:GT * P].rearrange("p (i c) -> p i c", c=P),
                                        bc(b1_bc[0:NT, :], [NT, GT, P], 1), ALU.add).then_inc(tab_sum, 1)
                    if 1 <= g <= NG:
                        s, n, at = (g - 1) % 2, l * NG + g - 1, slice((g - 1) * GT, g * GT)
                        v.wait_ge(tab_hi, n + 1)
                        if g >= 3:
                            v.wait_ge(tab_done, n - 1)
                        V.tensor_tensor(tab_r1[0:NT, s, :, :], tab_f[0:NT, s, :, :], table[0:NT, at, 0, :],
                                        ALU.subtract).then_inc(tab_r, 1)
                    if g >= 2:
                        s, n, at = g % 2, l * NG + g - 2, slice((g - 2) * GT, (g - 1) * GT)
                        v.wait_ge(tab_mid, n + 1)
                        V.tensor_tensor(table[0:NT, at, 2, :], tab_r1[0:NT, s, :, :], table[0:NT, at, 1, :],
                                        ALU.subtract).then_inc(tab_done, 1)

                def cells(i, n, first=False, last=False):
                    if not last:
                        b, (u, tiles) = n // NU, UNITS[n % NU]
                        s, cnt = n % 2, l * SU + i * NU + n // 2
                        v.wait_ge(ids_in[s], 2 * DMA * (cnt + 1))
                        v.wait_ge(pre_ready[s], done(cnt))
                        for k in range(2):
                            V.tensor_scalar(pick[:, s, k, 0:tiles * P], ids_bc[:, s, k, 0:tiles * P], part[:, 0:1], None,
                                            ALU.is_equal).then_inc(pick_ready[s], 1)
                    if not (first and n < 3) and not (last and n > 2):
                        i3, n3 = unit(i, n - 3)
                        tiles, s, cnt = UNITS[n3 % NU][1], n3 % 2, l * SU + i3 * NU + n3 // 2
                        v.wait_ge(r1_ready[s], cnt + 1)
                        V.tensor_copy(msg3[:, s, 0:tiles, 1, :], msg_r1[:, s, 0:tiles, :]).then_inc(mid_ready[s], 1)
                    if not (first and n < 2) and not (last and n > 1):
                        i2, n2 = unit(i, n - 2)
                        b, (u, tiles) = n2 // NU, UNITS[n2 % NU]
                        s, cnt = n2 % 2, l * SU + i2 * NU + n2 // 2
                        v.wait_ge(agg_ready[s], done(cnt))
                        V.tensor_tensor(pick_t[:, s, 0:tiles, :], bc(lane[:, :], [P, tiles, P], 1),
                                        bc(recv[:, bass.ds((2 * i2 + b) * BT + u, tiles)], [P, tiles, P], 2),
                                        ALU.is_equal).then_inc(pick_t_ready[s], 1)
                    if not (first and n < 4) and not (last and n > 3):
                        i4, n4 = unit(i, n - 4)
                        if n4 % NU == NU - 1:
                            b = n4 // NU
                            cnt = l * SU + i4 * NU + n4 // 2
                            v.wait_ge(agg_ready[n4 % 2], done(cnt + 1))
                            V.reduce_sum(agg[:, bass.ds(2 * i4 + b, 1), :].rearrange("p o e -> p (o e)"),
                                         agg_ps[:, b, 0:3 * EH].rearrange("p (k e) -> p e k", e=EH),
                                         AX.X).then_inc(bucket_out[b], 1)

                over_units(v, cells, 4)

                more = v.value_load(trips[0:1, 0:1], min_val=1, max_val=NQ // 2 - 1)
                n_trips = more + 1
                v.wait_ge(bucket_out[0], done((l + 1) * NI))
                v.wait_ge(bucket_out[1], done((l + 1) * NI))

                def prepare(q, it, s):
                    v.wait_ge(g_ids_in[s], DMA * (it + 1))
                    v.wait_ge(g_pre_ready[s], done(it))
                    V.tensor_scalar(pick[:, s, 0, :], ids_bc[:, s, 0, :], part[:, 0:1], None,
                                    ALU.is_equal).then_inc(g_pick_ready[s], 1)
                    v.wait_ge(g_agg_ready[s], done(it))
                    V.tensor_tensor(pick_g[:, s, :, :], bc(lane[:, :], [P, TPQ, P], 1),
                                    bc(g_recv[:, bass.ds(q * TPQ, TPQ)], [P, TPQ, P], 2),
                                    ALU.is_equal).then_inc(g_pick_t_ready[s], 1)

                def add(q, it, s):
                    _, bucket = nc.values_load_multi_w_load_instructions(
                        tile_bucket[0:1, bass.ds(q * TPQ, TPQ)], engines=DVE_ONLY, min_val=0, max_val=NB - 1,
                        skip_runtime_bounds_check_because="a count of buckets that end before is 0 to NB - 1")
                    v.wait_ge(g_agg_ready[s], done(it + 1))
                    for k in range(TPQ):
                        if k:
                            v.wait_ge(g_added[s], done(it * TPQ + k))
                        else:
                            v.wait_ge(g_added[1 - s], done((it + s) * TPQ))
                        where = agg[:, bass.ds(bucket[k], 1), :].rearrange("p o e -> p (o e)")
                        V.tensor_tensor(where, where, agg_ps[:, s, k * EH:(k + 1) * EH], ALU.add).then_inc(g_added[s], 1)

                for s in range(2):
                    v.wait_ge(agg_ready[s], done((l + 1) * SU))
                prepare(0, l * n_trips, 0)
                with v.Fori(0, more) as j:
                    prepare(2 * j + 1, l * n_trips + j, 1)
                    add(2 * j, l * n_trips + j, 0)
                    prepare(2 * j + 2, l * n_trips + j + 1, 0)
                    add(2 * j + 1, l * n_trips + j, 1)
                prepare(2 * more + 1, l * n_trips + more, 1)
                add(2 * more, l * n_trips + more, 0)
                add(2 * more + 1, l * n_trips + more, 1)
                for g in range(NG):
                    v.wait_ge(agg_tr, done(l * NG + g + 1))
                    V.tensor_copy(aggT[0:EH, g * GT * NT:(g + 1) * GT * NT].rearrange("p (i c) -> p i c", c=NT),
                                  grp_ps[g % 2][0:EH, 0:GT * P].rearrange("p (i c) -> p i c", c=P)[:, :, 0:NT],
                                  ).then_inc(aggT_ready, 1)
                with v.Fori(0, NI) as c:
                    for s in range(2):
                        v.wait_ge(upd_ps[s], done(l * NI + c + 1))
                        h_at = hT[:, bass.ds((2 * c + s) * NT, NT)]
                        V.scalar_tensor_tensor(h_at, psum[:, 6 + s, 0:NT], c2_sb[:, 0:1], h_at,
                                               ALU.add, ALU.add).then_inc(h_ready, 1)

            v.wait_ge(x_back, DMA)
            for g in range(NG):
                at = slice(g * GT, (g + 1) * GT)
                v.wait_ge(o_ps, g + 1)
                V.tensor_tensor(y[0:NT, at, :], grp_ps[g % 2][0:NT, 0:GT * F].rearrange("p (i f) -> p i f", f=F),
                                x_fin[0:NT, at, :], ALU.add).then_inc(o_out, 1)
            v.wait_ge(o_out, NG)
            Y, SQ, ST = y[0:NT, :, :], sq[0:NT, :, :], stat[0:NT, :, :]
            step(V.tensor_tensor(Y, Y, bc(b_out_bc[0:NT, :], [NT, NB, F], 1), ALU.add))
            step(V.reduce_sum(ST[:, 0, :], Y, AX.X))
            step(V.tensor_scalar(ST[:, 0, :], ST[:, 0, :], 1.0 / F, None, ALU.mult))
            step(V.tensor_tensor(Y, Y, bc(ST[:, 0, :], [NT, NB, F], 2), ALU.subtract))
            step(V.tensor_tensor(SQ, Y, Y, ALU.mult))
            step(V.reduce_sum(ST[:, 1, :], SQ, AX.X))
            V.tensor_scalar(ST[:, 1, :], ST[:, 1, :], 1.0 / F, 1e-5, ALU.mult, ALU.add).then_inc(fin_step, 1)
            v.wait_ge(sqrt_done, 1)
            step(V.reciprocal(ST[:, 3, :], ST[:, 2, :]))
            V.tensor_tensor(Y, Y, bc(ST[:, 3, :], [NT, NB, F], 2), ALU.mult).then_inc(o_ready, 1)

        @block.scalar
        def _(act):
            A = nc.scalar
            for s_ in (*s1_ready, *u_ready, *g_s1_ready, *g_msg_ready):
                act.sem_inc(s_, done(0))
            act.wait_ge(consts, N_CONSTS)
            for to, frm in ((src_raw, src), (dst_raw, dst)):
                act.dma_start(to[0:P - 1, :], frm[0:(P - 1) * NC].rearrange("(p c) -> p c", c=NC)).then_inc(edges_in, DMA)
                act.dma_start(to[P - 1:P, 0:CTAIL], frm[(P - 1) * NC:E].rearrange("(p c) -> p c", p=1)).then_inc(edges_in, DMA)
            for g in range(NG):
                s = g % 2
                act.wait_ge(x_tr, g + 1)
                if g >= 2:
                    act.wait_ge(h0_ps, g - 1)
                A.copy(xT[:, s, :].rearrange("f (i c) -> f i c", c=NT),
                       xt_ps[s][0:F, 0:GT * P].rearrange("f (i c) -> f i c", c=P)[:, :, 0:NT]).then_inc(x_tr_out, 1)
                act.wait_ge(h0_ps, g + 1)
                A.activation(hT[:, g * GT * NT:(g + 1) * GT * NT].rearrange("h (i c) -> h i c", c=NT),
                             grp_ps[s][:, 0:GT * P].rearrange("h (i c) -> h i c", c=P)[:, :, 0:NT],
                             ACT.Identity, bias=b_in_sb[:, 0:1]).then_inc(h_ready, GT)
            def batch(j, s, first_time=False):
                if not first_time:
                    act.wait_ge(scattered[s], DMA * SB * j)
                at = bass.ds((2 * j + s) * SB, SB)
                A.copy(rec_stage[:, s, :, 0], src_raw[:, at]).then_inc(staged[s], 1)
                A.copy(rec_stage[:, s, :, 1], dst_raw[:, at]).then_inc(staged[s], 1)

            act.wait_ge(look_ready, 1)
            for s in range(2):
                batch(0, s, first_time=True)
            with act.Fori(1, NBAT // 2) as j:
                for s in range(2):
                    batch(j, s)
            act.wait_ge(sorted_, 4)
            more = act.value_load(trips[0:1, 0:1], min_val=1, max_val=NQ // 2 - 1)
            n_trips = more + 1
            with act.Fori(0, L) as l:
                for g in range(NG + 1):
                    if g < NG:
                        act.wait_ge(tab_sum, l * NG + g + 1)
                        A.copy(table[0:NT, g * GT:(g + 1) * GT, 0, :], tab_f[0:NT, g % 2, :, :]).then_inc(tab_hi, 1)
                    if g:
                        act.wait_ge(tab_r, l * NG + g)
                        A.copy(table[0:NT, (g - 1) * GT:g * GT, 1, :], tab_r1[0:NT, (g - 1) % 2, :, :]).then_inc(tab_mid, 1)
                def stage_indices(q, it, s):
                    act.wait_ge(g_pre_ready[s], done(it))
                    A.copy(idx_stage[:, s, :], g_dst[:, bass.ds(q * TPQ, TPQ)]).then_inc(g_idx_ready[s], 1)

                for s in range(2):
                    act.wait_ge(table_out[s], DMA * (NG // 2) * (l + 1))
                for s in range(2):
                    stage_indices(s, l * n_trips, s)
                act.wait_ge(tab_done, (l + 1) * NG)

                def bucket_rows(i, b):
                    A.copy(rows[0:NT, b, :, :], table[0:NT, bass.ds(2 * i + b, 1), :, 0:EH]
                           .rearrange("p o k e -> p (o k) e")).then_inc(rows_ready[b], 1)

                def cells(i, n, first=False, last=False):
                    if not last:
                        s, cnt = n % 2, l * SU + i * NU + n // 2
                        tiles = UNITS[n % NU][1]
                        act.wait_ge(pre_ready[s], done(cnt + 1))
                        act.wait_ge(z_ready[s], done(cnt))
                        A.activation(s1[:, s, 0:tiles // 2 * P], pre_ps[:, s, 0:tiles // 2 * P],
                                     ACT.Silu).then_inc(s1_ready[s], 1)
                        if n % NU == NU - 1:
                            bucket_rows(i + 1, n // NU)
                    if not (first and n < 1) and not (last and n > 0):
                        i1, n1 = unit(i, n - 1)
                        tiles, s, cnt = UNITS[n1 % NU][1], n1 % 2, l * SU + i1 * NU + n1 // 2
                        act.wait_ge(z_ready[s], done(cnt + 1))
                        act.wait_ge(agg_ready[s], done(cnt))
                        A.activation(msg[:, s, 0:tiles, :].rearrange("p t e -> p (t e)"), z_ps[:, s, 0:tiles * EH],
                                     ACT.Silu).then_inc(msg_set, 1)
                        m1 = l * 2 * SU + i1 * 2 * NU + n1
                        act.wait_ge(msg_set, m1 + 1)
                        A.copy(msg3[:, s, 0:tiles, 0, :], msg[:, s, 0:tiles, :]).then_inc(hi_ready[s], 1)

                for b in range(2):
                    bucket_rows(0, b)
                over_units(act, cells, 1)

                def stage_rows(q, it, s):
                    _, bucket = nc.values_load_multi_w_load_instructions(
                        tile_bucket[0:1, bass.ds(q * TPQ, TPQ)], engines=ACT_ONLY, min_val=0, max_val=NB - 1,
                        skip_runtime_bounds_check_because="a count of buckets that end before is 0 to NB - 1")
                    for k in range(TPQ):
                        A.copy(rows_g[0:NT, s, k, :, :],
                               table[0:NT, bass.ds(bucket[k], 1), :, 0:EH].rearrange("p o k e -> p (o k) e"),
                               ).then_inc(g_rows_ready[s], 1)

                def silus(it, s, ahead=None):
                    act.wait_ge(g_pre_ready[s], done(it + 1))
                    act.wait_ge(g_z_ready[s], done(it))
                    A.activation(s1[:, s, :], pre_ps[:, s, :], ACT.Silu).then_inc(g_s1_ready[s], 1)
                    if ahead is not None:
                        stage_indices(ahead, it + 1, s)
                    act.wait_ge(g_z_ready[s], done(it + 1))
                    act.wait_ge(g_agg_ready[s], done(it))
                    A.activation(msg[:, s, :, :].rearrange("p t e -> p (t e)"), z_ps[:, s, :],
                                 ACT.Silu).then_inc(g_msg_ready[s], 1)
                    if ahead is not None:
                        stage_rows(ahead, it + 1, s)

                for s in range(2):
                    stage_rows(s, l * n_trips, s)
                for s in range(2):
                    act.wait_ge(agg_ready[s], done((l + 1) * SU))
                with act.Fori(0, more) as j:
                    for s in range(2):
                        silus(l * n_trips + j, s, ahead=2 * j + 2 + s)
                for s in range(2):
                    silus(l * n_trips + more, s)
                with act.Fori(0, NI) as c:
                    for s in range(2):
                        act.wait_ge(u_ps_ready[s], l * NI + c + 1)
                        act.wait_ge(upd_ps[s], done(l * NI + c))
                        A.activation(u_sb[:, s, :], psum[:, 4 + s, 0:NT], ACT.Silu,
                                     bias=c1_sb[:, 0:1]).then_inc(u_ready[s], 1)
            act.wait_ge(fin_step, 1)
            A.activation(stat[0:NT, 2, :], stat[0:NT, 1, :], ACT.Sqrt).then_inc(sqrt_done, 1)

        @block.tensor
        def _(pe):
            def mm(o, a, b, start=True, stop=True):
                return nc.tensor.matmul(o, a, b, start=start, stop=stop)

            for s_ in (*pre_ready, *z_ready, *agg_ready, *upd_ps, *g_pre_ready, *g_z_ready, *g_agg_ready, agg_tr,
                       *c_used):
                pe.sem_inc(s_, done(0))
            pe.wait_ge(seq, 14)
            pe.wait_ge(loaded, DMA * 5)
            for g in range(NG):
                s = g % 2
                if g >= 2:
                    pe.wait_ge(h_ready, (g - 1) * GT)
                for i in range(GT):
                    last = mm(xt_ps[s][0:F, i * P:i * P + NT], x_sb[0:NT, g * GT + i, :], ident[0:NT, 0:NT])
                last.then_inc(x_tr, 1)
                pe.wait_ge(x_tr_out, g + 1)
                for i in range(GT):
                    last = mm(grp_ps[s][:, i * P:i * P + NT], W_in_sb[:, :], xT[:, s, i * NT:(i + 1) * NT])
                last.then_inc(h0_ps, 1)
            pe.wait_ge(h_ready, NB)

            def transpose(k, a, r, n, i):
                pe.wait_ge(t_ready, k)
                if k > 1:
                    pe.wait_ge(t_copied, k - 1)
                for m in range(n):
                    last = mm(t_ps[0:r, m * P:(m + 1) * P], a[:, m * r:(m + 1) * r], i[:, :])
                last.then_inc(t_done, 1)

            transpose(1, cell, CB, NC // CB, ident)
            pe.wait_ge(t_copied, 1)
            for m in range(NC // CB):
                last = mm(t_ps[0:CB, m * P:(m + 1) * P], dtile[:, m * CB:(m + 1) * CB], ident_b[:, :])
            last.then_inc(t_done, 1)
            Z = zeros_b[:, 0:NB]
            mm(cnt_ps, Z, Z, stop=False)
            with pe.Fori(0, NBAT // 2) as j:
                for s in range(2):
                    pe.wait_ge(c_oh[s], 2 * (j + 1))
                    for c in range(SB):
                        last = mm(cnt_ps, oh_dt[:, s, c, :], oh_st[:, s, c, :], start=False, stop=False)
                    last.then_inc(c_used[s], 1)
            mm(cnt_ps, Z, Z, start=False).then_inc(counted, 1)
            pe.wait_ge(excess_ready, 1)
            mm(exc_ps[:, 0:NB], ones[0:NB, :], excess[:, :]).then_inc(summed, 1)
            mm(exc_ps[0:NB, P:P + NB], tri[0:NB, 0:NB], excess[:, :]).then_inc(summed, 1)
            pe.wait_ge(look_ready, 1)
            with pe.Fori(0, NBAT // 2) as j:
                for s in range(2):
                    pe.wait_ge(oh_ready[s], 3 * (j + 1))
                    for g in range(GPB):
                        c0 = 2 * g
                        k = min(2, SB - c0)
                        gs = (s * GPB + g) % 2
                        n = (2 * j + s) * GPB + g
                        for m in range(k):
                            last = mm(group_ps[gs], oh_dt[:, s, c0 + m, :], oh_st[:, s, c0 + m, :],
                                      start=m == 0, stop=m == k - 1)
                        last.then_inc(grouped, 1)
                        pe.wait_ge(count_set, done(n))
                        pe.wait_ge(look_read, n if s + g else done(n))
                        for m in range(k):
                            last = mm(look_ps[:, gs, m * 2 * NB:(m + 1) * 2 * NB], oh_d[:, s, (c0 + m) * P:(c0 + m + 1) * P],
                                      look[:, gs, :, :].rearrange("p w i -> p (w i)"))
                        last.then_inc(looked, 1)
            transpose(3, recv, RBF, FASTT // RBF, ident_b)
            transpose(4, rb, RBF, FASTT // RBF, ident_b)
            transpose(5, g_recv, RBG, T // RBG, ident_b)
            pe.wait_ge(sorted_, 4)

            with pe.Fori(0, L) as l:
                pe.wait_ge(weights, DMA * N_WEIGHTS * (l + 1))
                pe.wait_ge(h_ready, (l + 1) * NB)
                for g in range(NG):
                    if g >= 2:
                        pe.wait_ge(tab_sum, l * NG + g - 1)
                    for i in range(GT):
                        n = g * GT + i
                        last = mm(grp_ps[g % 2][0:NT, i * P:(i + 1) * P], hT[:, n * NT:(n + 1) * NT], w1_sb[:, :])
                    last.then_inc(tab_ps, 1)
                pe.wait_ge(tab_done, (l + 1) * NG)
                pe.wait_ge(b2_step, 8 * (l + 1))

                def before_silu(i, n):
                    b, (u, tiles) = n // NU, UNITS[n % NU]
                    s, cnt, half = n % 2, l * SU + i * NU + n // 2, tiles // 2 * P
                    pe.wait_ge(s1_ready[s], done(cnt))
                    pe.wait_ge(pick_ready[s], done(2 * (cnt + 1)))
                    pe.wait_ge(rows_ready[b], l * (NI + 1) + i + 1)
                    at = pieces(tiles, u)
                    ends = {h: max(k for k, p in enumerate(at) if p[0] == h) for h in range(2)
                            if any(p[0] == h for p in at)}
                    for k in range(3):
                        for h in range(2):
                            mm(pre_ps[h * EH:(h + 1) * EH, s, 0:half], rows[0:NT, b, k, :],
                               pick[0:NT, s, 0, h * half:(h + 1) * half], start=k == 0, stop=k == 2 and h not in ends)
                    for m, (h, c0, w, d) in enumerate(at):
                        for k in range(3):
                            last = mm(pre_ps[h * EH:(h + 1) * EH, s, c0:c0 + w], table[0:NT, d, k, EH:P],
                                      pick[0:NT, s, 1, h * half + c0:h * half + c0 + w],
                                      start=False, stop=k == 2 and m == ends[h])
                    last.then_inc(pre_ready[s], 1)

                def second(i, n):
                    tiles, s, cnt = UNITS[n % NU][1], n % 2, l * SU + i * NU + n // 2
                    pe.wait_ge(s1_ready[s], done(cnt + 1))
                    mm(z_ps[:, s, 0:tiles * EH], ones_b[:, :],
                       b2_parts[:, 0:tiles, :].rearrange("p t e -> p (t e)"), stop=False)
                    for k in range(tiles // 2):
                        last = mm(z_ps[:, s, k * P:(k + 1) * P], s1[:, s, k * P:(k + 1) * P], w2_sb[:, :],
                                  start=False, stop=k == tiles // 2 - 1)
                    last.then_inc(z_ready[s], 1)

                def sums(i, n):
                    b, (u, tiles) = n // NU, UNITS[n % NU]
                    s, cnt = n % 2, l * SU + i * NU + n // 2
                    pe.wait_ge(pick_t_ready[s], cnt + 1)
                    pe.wait_ge(msg3_ready[s], cnt + 1)
                    if u == 0:
                        pe.wait_ge(bucket_out[b], done(l * NI + i))
                    for m in range(tiles):
                        t = m // 2 + (m % 2) * (tiles // 2)
                        last = mm(agg_ps[:, b, 0:3 * EH], pick_t[:, s, t, :],
                                  msg3[:, s, m, :, :].rearrange("p k e -> p (k e)"),
                                  start=u + m == 0, stop=u + m == BT - 1)
                    last.then_inc(agg_ready[s], 1)

                def cells(i, n, first=False, last=False):
                    if not last:
                        before_silu(i, n)
                    if not (first and n < 3):
                        sums(*unit(i, n - 3))
                    if not (first and n < 1) and not (last and n > 0):
                        second(*unit(i, n - 1))

                over_units(pe, cells, 3)

                more = pe.value_load(trips[0:1, 0:1], min_val=1, max_val=NQ // 2 - 1)
                n_trips = more + 1
                for s in range(2):
                    pe.wait_ge(s1_ready[s], done((l + 1) * SU))
                    pe.wait_ge(bucket_out[s], done((l + 1) * NI))
                pe.sem_inc(turn, 1)
                with pe.Fori(0, n_trips) as j:
                    for s in range(2):
                        it = l * n_trips + j
                        pe.wait_ge(gathered[s], DMA * TPQ * (it + 1))
                        pe.wait_ge(g_s1_ready[s], done(it))
                        for k in range(PPQ):
                            mm(pre_ps[:, s, k * P:(k + 1) * P], gath[:, s, k * P:(k + 1) * P], ident[:, :],
                               start=k == 0, stop=False)
                        pe.wait_ge(g_pick_ready[s], done(it + 1))
                        pe.wait_ge(g_rows_ready[s], TPQ * (it + 1))
                        for k in range(PPQ):
                            for p3 in range(3):
                                for h in range(2):
                                    t = 2 * k + h
                                    last = mm(pre_ps[h * EH:(h + 1) * EH, s, k * P:(k + 1) * P],
                                              rows_g[0:NT, s, t, p3, :], pick[0:NT, s, 0, t * P:(t + 1) * P],
                                              start=False, stop=k == PPQ - 1 and p3 == 2)
                        last.then_inc(g_pre_ready[s], 1)
                        pe.wait_ge(g_msg_ready[s], done(it))
                        mm(z_ps[:, s, :], ones_b[:, :], b2_parts[:, :, :].rearrange("p t e -> p (t e)"), stop=False)
                        pe.wait_ge(g_s1_ready[s], done(it + 1))
                        for k in range(PPQ):
                            last = mm(z_ps[:, s, k * P:(k + 1) * P], s1[:, s, k * P:(k + 1) * P], w2_sb[:, :],
                                      start=False, stop=k == PPQ - 1)
                        last.then_inc(g_z_ready[s], 1)
                        pe.wait_ge(g_added[s], done(TPQ * it))
                        pe.wait_ge(g_pick_t_ready[s], it + 1)
                        pe.wait_ge(g_msg_ready[s], done(it + 1))
                        for t in range(TPQ):
                            last = mm(agg_ps[:, s, t * EH:(t + 1) * EH], pick_g[:, s, t, :], msg[:, s, t, :])
                        last.then_inc(g_agg_ready[s], 1)
                for s in range(2):
                    pe.wait_ge(g_added[s], done(TPQ * n_trips * (l + 1)))
                for g in range(NG):
                    if g >= 2:
                        pe.wait_ge(aggT_ready, l * NG + g - 1)
                    for i in range(GT):
                        last = mm(grp_ps[g % 2][0:EH, i * P:i * P + NT], agg[0:NT, g * GT + i, :], ident[0:NT, 0:NT])
                    last.then_inc(agg_tr, 1)
                pe.wait_ge(aggT_ready, (l + 1) * NG)
                pe.sem_inc(turn, 1)
                with pe.Fori(0, NI) as c:
                    for s in range(2):
                        pe.wait_ge(u_ready[s], done(l * NI + c))
                        at = bass.ds((2 * c + s) * NT, NT)
                        mm(psum[:, 4 + s, 0:NT], m1h_sb[:, :], hT[:, at], stop=False)
                        mm(psum[:, 4 + s, 0:NT], m1a_sb[:, :], aggT[0:EH, at], start=False).then_inc(u_ps_ready[s], 1)
                    for s in range(2):
                        pe.wait_ge(u_ready[s], done(l * NI + c + 1))
                        pe.wait_ge(h_ready, (l + 1) * NB + 2 * c + s - 1)
                        mm(psum[:, 6 + s, 0:NT], m2_sb[:, :], u_sb[:, s, :]).then_inc(upd_ps[s], 1)
            pe.wait_ge(h_ready, (L + 1) * NB)
            for g in range(NG):
                if g >= 2:
                    pe.wait_ge(o_out, g - 1)
                for i in range(GT):
                    n = g * GT + i
                    last = mm(grp_ps[g % 2][0:NT, i * F:(i + 1) * F], hT[:, n * NT:(n + 1) * NT], W_out_sb[:, :])
                last.then_inc(o_ps, 1)


_INS = ['x', 'src', 'dst'] + ['L0_gnn_' + n for n in
                              ('W_in', 'b_in', 'eW1', 'eb1', 'eW2', 'eb2', 'nW1', 'nb1', 'nW2', 'nb2', 'W_out', 'b_out')]


def kernel(**inputs):
    import numpy as _np
    import concourse.bacc as _bacc
    from concourse import mybir as _mybir
    from concourse.bass_utils import run_bass_kernel_spmd as _run

    nc = _bacc.Bacc("TRN2", target_bir_lowering=False, num_devices=1)
    arrays, args = {}, []
    for name in _INS:
        a = _np.ascontiguousarray(inputs[name])
        arrays[f"in_{name}_dram"] = a
        args.append(nc.dram_tensor(f"in_{name}_dram", a.shape, _mybir.dt.from_np(a.dtype), kind="ExternalInput").ap())
    shape = tuple(arrays["in_x_dram"].shape)
    args.append(nc.dram_tensor("out_dram", shape, _mybir.dt.float32, kind="ExternalOutput").ap())
    build_gnn(nc, *args)
    r = _run(nc, [arrays], core_ids=[0])
    return r.results[0]["out_dram"]
```

```python
import concourse.bass as bass
from concourse import mybir
from contextlib import ExitStack

F32 = mybir.dt.float32
BF16 = mybir.dt.bfloat16
I32 = mybir.dt.int32
ALU = mybir.AluOpType
ACT = mybir.ActivationFunctionType
AX = mybir.AxisListType
DVE_ONLY = [mybir.EngineType.DVE]
ACT_ONLY = [mybir.EngineType.Activation]

P = 128
TPQ = 8
PPQ = TPQ // 2
GU = 4
DMA = 16
ROUND = 12582912.0


def done(n):
    return n + 1


def divisor(n, most, even_count=False):
    return max(d for d in range(1, most + 1) if n % d == 0 and not (even_count and (n // d) % 2))


def build_gnn(nc, x, src, dst, W_in, b_in, eW1, eb1, eW2, eb2, nW1, nb1, nW2, nb2, W_out, b_out, out):
    N, F = x.shape
    E = src.shape[0]
    H = W_in.shape[1]
    L, _, EH = eW1.shape
    assert H == P and EH * 2 == P and F == EH
    NT = divisor(N, P)
    NB = N // NT
    GT = divisor(NB, 5, even_count=True)
    NG = NB // GT
    CW = 512 // NT * NT
    CHUNKS = [(n, min(CW, N - n)) for n in range(0, N, CW)]
    NCH = len(CHUNKS)
    NI = NB // 2
    NC = -(-E // P)
    CTAIL = E - (P - 1) * NC
    assert 0 < CTAIL <= NC and NC - CTAIL <= P
    SB = divisor(NC, 16, even_count=True)
    NBAT = NC // SB
    ENDS = -(-(NB - 1) // (NBAT // 2))
    GPB = -(-SB // 2)
    CB = divisor(NC, P)
    MEAN = max(E - N, 0) / NB ** 2
    BT = -(-(int(MEAN + MEAN ** 0.5 / 2) * NB + NT) // P)
    BT += BT % 2
    C = (BT * P - NT) // NB
    FASTT = NB * BT
    UNITS = [(u, min(TPQ, BT - u)) for u in range(0, BT, TPQ)]
    NU = len(UNITS)
    AHEAD = min(NI - 1, -(-GU * TPQ // (2 * NU)))
    NQ = -(-((E + NB * (P - 1)) // P) // TPQ)
    NQ += -NQ % GU
    TRIP_BITS = (GU * TPQ).bit_length() - 1
    T = NQ * TPQ
    TT = FASTT + 1 + T
    RBF, RBG = divisor(FASTT, P), divisor(T, P)

    def pieces(tiles, first):
        half = tiles // 2 * P
        cells = [(d * C, (d + 1) * C, d) for d in range(NB)] + [(NB * C, NB * C + NT, NB)]
        found = ([], [])
        for h in range(2):
            at = first * P + h * half
            for q0, q1, d in cells:
                q0, q1 = max(q0, at), min(q1, at + half)
                if q0 < q1:
                    found[h].append((h, q0 - at, q1 - q0, d))
        both = []
        for k in range(max(map(len, found))):
            both += [f[k] for f in found if k < len(f)]
        return both

    records = nc.dram_tensor("records", (P * TT, 2), I32).ap()
    cell_rows = nc.dram_tensor("cell_rows", (NC, P), F32).ap()
    dtile_rows = nc.dram_tensor("dtile_rows", (NC, P), BF16).ap()
    src_rows_d = nc.dram_tensor("src_rows_d", (FASTT, P), BF16).ap()
    dst_rows_d = nc.dram_tensor("dst_rows_d", (FASTT, P), BF16).ap()
    gen_rows_d = nc.dram_tensor("gen_rows_d", (T, P), BF16).ap()
    dst_table = nc.dram_tensor("dst_table", (N, EH), F32).ap()

    with ExitStack() as ctx:
        def sb(name, shape, dt, c=ctx):
            return c.enter_context(nc.sbuf_tensor(name, shape, dt))

        def sem(name, n=0):
            if n:
                return [ctx.enter_context(nc.semaphore(f"{name}{k}")) for k in range(n)]
            return ctx.enter_context(nc.semaphore(name))

        ident = sb("ident", [P, P], F32)
        ident_b = sb("ident_b", [P, P], BF16)
        ones_b = sb("ones_b", [P, P], BF16)
        zeros_b = sb("zeros_b", [P, P], BF16)
        part = sb("part", [P, 1], F32)
        lane = sb("lane", [P, P], F32)
        pick3 = sb("pick3", [P, 3], F32)

        W_in_sb = sb("W_in_sb", [F, H], F32)
        b_in_sb = sb("b_in_sb", [H, 1], F32)
        w1_sb = sb("w1_sb", [H, P], F32)
        b1_bc = sb("b1_bc", [P, P], F32)
        w2_sb = sb("w2_sb", [P, P], F32)
        b2_bc = sb("b2_bc", [P, EH], F32)
        b2_hi = sb("b2_hi", [P, EH], BF16)
        b2_mid = sb("b2_mid", [P, EH], BF16)
        b2_r1 = sb("b2_r1", [P, EH], F32)
        b2_r2 = sb("b2_r2", [P, EH], F32)
        b2_sum = sb("b2_sum", [P, EH], F32)
        b2_parts = sb("b2_parts", [P, TPQ, EH], BF16)
        m1h_sb = sb("m1h_sb", [H, H], F32)
        m1a_sb = sb("m1a_sb", [EH, H], F32)
        c1_sb = sb("c1_sb", [H, 1], F32)
        m2_sb = sb("m2_sb", [H, H], F32)
        c2_sb = sb("c2_sb", [H, 1], F32)
        W_out_sb = sb("W_out_sb", [H, F], F32)
        b_out_bc = sb("b_out_bc", [P, F], F32)

        hT = sb("hT", [H, N], F32)
        recv = sb("recv", [P, FASTT], BF16)
        g_recv = sb("g_recv", [P, T], BF16)
        g_dst = sb("g_dst", [P, T], I32)
        tile_bucket = sb("tile_bucket", [P, T], I32)
        trips = sb("trips", [P, 1], I32)

        with ExitStack() as early:
            tri = sb("tri", [P, P], F32, early)
            ones = sb("ones", [P, P], F32, early)
            before = sb("before", [P, 2, 2 * P], F32, early)
            tile_i = sb("tile_i", [P, NB], F32, early)
            col_no = sb("col_no", [P, NC], F32, early)
            x_sb = sb("x_sb", [P, NB, F], F32, early)
            xT = sb("xT", [F, 2, GT * NT], F32, early)
            src_raw = sb("src_raw", [P, NC], I32, early)
            dst_raw = sb("dst_raw", [P, NC], I32, early)
            stile = sb("stile", [P, NC], BF16, early)
            dtile = sb("dtile", [P, NC], BF16, early)
            cell = sb("cell", [P, NC], F32, early)
            base = sb("base", [P, NC], F32, early)
            room = sb("room", [P, NC], F32, early)
            tmp1 = sb("tmp1", [P, NC], F32, early)
            tmp2 = sb("tmp2", [P, NC], F32, early)
            cell_t = sb("cell_t", [CB, NC // CB, P], F32, early)
            dtile_t = sb("dtile_t", [CB, NC // CB, P], BF16, early)
            cell_bc = sb("cell_bc", [P, 2, SB * P], F32, early)
            dtile_bc = sb("dtile_bc", [NB, 2, SB * P], BF16, early)
            oh_d = sb("oh_d", [NB, 2, SB * P], F32, early)
            oh_dt = sb("oh_dt", [P, 2, SB, NB], BF16, early)
            oh_st = sb("oh_st", [P, 2, SB, NB], BF16, early)
            look = sb("look", [NB, 2, 2, NB], F32, early)
            prod = sb("prod", [P, 2, 2, 2, NB], F32, early)
            eq = sb("eq", [P, 2, 2, 2 * P], F32, early)
            r_cell = sb("r_cell", [P, 2, 2 * GPB, 2], F32, early)
            r_in = sb("r_in", [P, 2, SB], F32, early)
            f_d = sb("f_d", [P, SB], F32, early)
            f_r = sb("f_r", [P, SB], F32, early)
            f_m = sb("f_m", [P, SB], F32, early)
            f_v = sb("f_v", [P, SB], F32, early)
            f_t = sb("f_t", [P, SB], F32, early)
            f_u = sb("f_u", [P, SB], F32, early)
            f_lin = sb("f_lin", [P, SB], I32, early)
            f_lo = sb("f_lo", [P, SB], I32, early)
            f_hi = sb("f_hi", [P, SB], I32, early)
            pos_stage = sb("pos_stage", [P, 2, SB], I32, early)
            rec_stage = sb("rec_stage", [P, 2, SB, 2], I32, early)
            excess = sb("excess", [NB, NB], F32, early)
            tot_i = sb("tot_i", [P, NB], I32, early)
            ntile_i = sb("ntile_i", [P, NB], I32, early)
            ntile = sb("ntile", [P, NB], F32, early)
            tile_end = sb("tile_end", [P, max(NB, ENDS * (NBAT // 2))], F32, early)
            first = sb("first", [P, NB], F32, early)
            trips_i = sb("trips_i", [P, 2], I32, early)
            PADT = 512
            pads = sb("pads", [P, PADT, 2], I32, early)
            tile_f = sb("tile_f", [P, T], F32, early)
            tile_no = sb("tile_no", [P, T], F32, early)
        with ExitStack() as mid:
            recs = sb("recs", [P, max(FASTT, T), 2], I32, mid)
            rf = sb("rf", [P, FASTT], F32, mid)
            rt = sb("rt", [P, FASTT], F32, mid)
            rb = sb("rb", [P, FASTT], BF16, mid)
            rows_t = sb("rows_t", [P, 2560], BF16, mid)

        aggT = sb("aggT", [P, max(N, 2 * NB * F)], F32)
        x_fin = aggT[:, 0:NB * F].rearrange("p (i f) -> p i f", f=F)
        sq = aggT[:, NB * F:2 * NB * F].rearrange("p (i f) -> p i f", f=F)
        agg = sb("agg", [P, NB, EH], F32)
        y = agg
        table = sb("table", [P, NB + 2, 3, P], BF16)
        tab_f = sb("tab_f", [P, 2, GT, P], F32)
        tab_r1 = sb("tab_r1", [P, 2, GT, P], F32)
        ids_bc = sb("ids_bc", [P, 2, 2, TPQ * P], BF16)
        pick = sb("pick", [P, 2, 2, TPQ * P], BF16)
        pick_g = sb("pick_g", [P, 2, TPQ, P], F32)
        pick_t = pick_g[:, :, 0:TPQ // 2, :].rearrange("p s t n -> p s (t n)").bitcast(BF16).rearrange(
            "p s (t n) -> p s t n", n=P)
        rows = sb("rows", [P, 2, 3, P], BF16)
        rows_g = sb("rows_g", [P, 2, TPQ, 3, EH], BF16)
        idx_stage = sb("idx_stage", [P, GU, TPQ], I32)
        gath = sb("gath", [P, GU, TPQ * EH], F32)
        s1 = sb("s1", [P, 2, PPQ * P], F32)
        msg = sb("msg", [P, 2, TPQ, EH], F32)
        msg_r1 = sb("msg_r1", [P, 2, TPQ, EH], F32)
        msg3 = sb("msg3", [P, 2, TPQ, 3, EH], BF16)
        u_sb = sb("u_sb", [H, 2, CW], F32)
        stat = sb("stat", [P, 4, NB], F32)

        psum = ctx.enter_context(nc.psum_tensor("psum", [P, 8, 512], F32))

        def bank2(k):
            return psum[:, k:k + 2, :].rearrange("p b c -> p (b c)")

        pre_ps = psum[:, 0:2, :]
        z_ps = psum[:, 2:4, :]
        agg_ps = psum[:, 4:6, :]
        grp_ps = [bank2(0), bank2(2)]
        xt_ps = [bank2(4), bank2(6)]
        t_ps = psum[:, 3:8, :].rearrange("p b c -> p (b c)")
        cnt_ps = psum[0:NB, 0, 0:NB]
        look_ps = psum[:, 1:3, :]
        group_ps = [psum[0:NB, 4 + k, 0:NB] for k in range(2)]
        exc_ps = psum[:, 3, :]

        loaded, edges_in, consts = sem("loaded"), sem("edges_in"), sem("consts")
        turn = sem("turn")
        padded, pad_set = sem("padded"), sem("pad_set")
        seq = sem("seq")
        x_tr, x_tr_out, h0_ps, h_ready = sem("x_tr"), sem("x_tr_out"), sem("h0_ps"), sem("h_ready")
        t_ready = sem("t_ready")
        t_done = sem("t_done")
        t_copied = sem("t_copied")
        t_out = sem("t_out")
        cells_out = sem("cells_out")
        c_oh = sem("c_oh", 2)
        c_used = sem("c_used", 2)
        counted = sem("counted")
        excess_ready, summed, look_ready = sem("excess_ready"), sem("summed"), sem("look_ready")
        bc_in = sem("bc_in", 2)
        oh_ready = sem("oh_ready", 2)
        looked = sem("looked")
        grouped = sem("grouped")
        count_set = sem("count_set")
        look_read = sem("look_read")
        ranked = sem("ranked")
        placed = sem("placed")
        staged = sem("staged", 2)
        scattered = sem("scattered", 2)
        recs_in = sem("recs_in")
        sorted_ = sem("sorted")
        tile_step = sem("tile_step")
        weights, node_weights, b2_step = sem("weights"), sem("node_weights"), sem("b2_step")
        tab_ps, tab_sum, tab_hi, tab_r, tab_mid, tab_done = (sem(n) for n in
            ("tab_ps", "tab_sum", "tab_hi", "tab_r", "tab_mid", "tab_done"))
        table_out = sem("table_out", 2)
        ids_in, pick_ready, pick_t_ready = sem("ids_in", 2), sem("pick_ready", 2), sem("pick_t_ready", 2)
        rows_ready, pre_ready, s1_ready, z_ready = (sem(n, 2) for n in ("rows_ready", "pre_ready", "s1_ready", "z_ready"))
        hi_ready, msg3_ready, agg_ready = sem("hi_ready", 2), sem("msg3_ready", 2), sem("agg_ready", 2)
        msg_set = sem("msg_set")
        bucket_out = sem("bucket_out", 2)
        r1_ready, mid_ready = sem("r1_ready", 2), sem("mid_ready", 2)
        g_ids_in, g_pick_ready, g_pick_t_ready = sem("g_ids_in", 2), sem("g_pick_ready", 2), sem("g_pick_t_ready", 2)
        g_rows_ready, g_idx_ready, gathered = sem("g_rows_ready", 2), sem("g_idx_ready", GU), sem("gathered", GU)
        g_pre_ready, g_s1_ready, g_z_ready = (sem(n, 2) for n in ("g_pre_ready", "g_s1_ready", "g_z_ready"))
        g_msg_ready, g_agg_ready, g_added = (sem(n, 2) for n in ("g_msg_ready", "g_agg_ready", "g_added"))
        agg_tr, aggT_ready = sem("agg_tr"), sem("aggT_ready")
        u_ps_ready, u_ready, upd_ps = sem("u_ps_ready"), sem("u_ready"), sem("upd_ps")
        x_back, o_ps, o_out, o_ready, fin_step, sqrt_done, stored = (sem(n) for n in
            ("x_back", "o_ps", "o_out", "o_ready", "fin_step", "sqrt_done", "stored"))

        N_WEIGHTS, N_NODE_WEIGHTS = 6, 5
        N_CONSTS = 7
        SU = NI * NU

        block = ctx.enter_context(nc.Block())

        def unit(i, n):
            return (i, n) if n >= 0 else (i - 1, n + 2 * NU)

        def over_units(eng, step, lag):
            for n in range(2 * NU):
                step(0, n, first=True)
            if NI > 1:
                with eng.Fori(1, NI) as i:
                    for n in range(2 * NU):
                        step(i, n)
            for n in range(lag):
                step(NI, n, last=True)

        def bc(ap, shape, *dims):
            for d in dims:
                ap = ap.unsqueeze(d)
            return ap.to_broadcast(shape)

        def groups(batches):
            return (batches + 1) * GPB + 1

        def nth(trip, u):
            return trip * (GU // 2) + u // 2

        @block.sync
        def _(sp):
            x_v = x.rearrange("(i p) f -> p i f", p=NT)
            sp.dma_start(x_sb[0:NT, :, :], x_v).then_inc(loaded, DMA)
            sp.dma_start(W_in_sb[:, :], W_in).then_inc(loaded, DMA)
            sp.dma_start(b_in_sb[:, :], b_in.rearrange("(h o) -> h o", o=1)).then_inc(loaded, DMA)
            sp.dma_start(W_out_sb[:, :], W_out).then_inc(loaded, DMA)
            sp.dma_start(b_out_bc[:, :], b_out.partition_broadcast(P)).then_inc(loaded, DMA)
            sp.wait_ge(pad_set, 2)
            records_v = records.rearrange("(p t) c -> p t c", p=P)
            for t in range(0, TT, PADT):
                n = min(PADT, TT - t)
                sp.dma_start(records_v[:, t:t + n, :], pads[:, 0:n, :]).then_inc(padded, DMA)
            sp.wait_ge(t_copied, 1)
            sp.dma_start(cell_rows.rearrange("(b r) p -> r b p", r=CB), cell_t[:, :, :]).then_inc(cells_out, DMA)
            sp.wait_ge(t_copied, 2)
            sp.dma_start(dtile_rows.rearrange("(b r) p -> r b p", r=CB), dtile_t[:, :, :]).then_inc(cells_out, DMA)
            sp.wait_ge(cells_out, 2 * DMA)
            with sp.Fori(0, NBAT // 2) as j:
                for s in range(2):
                    at = bass.ds((2 * j + s) * SB, SB)
                    sp.wait_ge(ranked, groups(2 * j + s - 1))
                    sp.dma_start(cell_bc[:, s, :], cell_rows[at, :].rearrange("t p -> (t p)").partition_broadcast(P)).then_inc(bc_in[s], DMA)
                    sp.dma_start(dtile_bc[:, s, :], dtile_rows[at, :].rearrange("t p -> (t p)").partition_broadcast(NB)).then_inc(bc_in[s], DMA)
            for s in range(2):
                sp.wait_ge(scattered[s], DMA * (NC // 2))
            sp.wait_ge(sorted_, 1)
            sp.dma_start(recs[:, 0:FASTT, :], records_v[:, 0:FASTT, :]).then_inc(recs_in, DMA)
            for k, (d, r) in enumerate(((src_rows_d, RBF), (dst_rows_d, RBF), (gen_rows_d, RBG))):
                sp.wait_ge(t_copied, 3 + k)
                n = d.shape[0] // r
                sp.dma_start(d.rearrange("(b r) p -> r b p", r=r),
                             rows_t[0:r, 0:n * P].rearrange("r (b p) -> r b p", p=P)).then_inc(t_out, DMA)
                if k == 0:
                    sp.wait_ge(sorted_, 2)
                    sp.dma_start(recs[:, 0:T, :], records_v[:, FASTT + 1:TT, :]).then_inc(recs_in, DMA)
            sp.wait_ge(t_out, 3 * DMA)
            more = sp.value_load(trips[0:1, 0:1], min_val=1, max_val=NQ // GU - 1)
            n_trips = more + 1
            with sp.Fori(0, L) as l:
                for s in range(2):
                    sp.wait_ge(g_agg_ready[s], done(nth(l * n_trips, 0)))
                sp.wait_ge(sorted_, 4)
                dl = bass.ds(l, 1)
                for to, frm in ((w1_sb[:, 0:EH], eW1[dl, 0:H, :]), (w1_sb[:, EH:P], eW1[dl, H:2 * H, :]),
                                (w2_sb[0:EH, 0:EH], eW2[dl, :, :]), (w2_sb[EH:P, EH:P], eW2[dl, :, :])):
                    sp.dma_start(to, frm.rearrange("o h e -> (o h) e")).then_inc(weights, DMA)
                for to, frm in ((b1_bc[:, EH:P], eb1), (b2_bc[:, :], eb2)):
                    sp.dma_start(to, frm[dl, :].rearrange("o e -> (o e)").partition_broadcast(P)).then_inc(weights, DMA)

                def ids(i, n, first=False, last=False):
                    b, (u, tiles) = n // NU, UNITS[n % NU]
                    s, cnt = n % 2, l * SU + i * NU + n // 2
                    sp.wait_ge(pick_ready[s], done(2 * cnt))
                    for k, d in enumerate((src_rows_d, dst_rows_d)):
                        sp.dma_start(ids_bc[:, s, k, 0:tiles * P],
                                     d[bass.ds((2 * i + b) * BT + u, tiles), :].rearrange("t p -> (t p)")
                                     .partition_broadcast(P)).then_inc(ids_in[s], DMA)

                for n in range(2):
                    ids(0, n)
                sp.wait_ge(h_ready, (l + 1) * NB)
                for to, frm in ((m1h_sb[:, :], nW1[dl, 0:H, :]), (m1a_sb[:, :], nW1[dl, H:H + EH, :]),
                                (m2_sb[:, :], nW2[dl, :, :])):
                    sp.dma_start(to, frm.rearrange("o h e -> (o h) e")).then_inc(node_weights, DMA)
                for to, frm in ((c1_sb, nb1), (c2_sb, nb2)):
                    sp.dma_start(to[:, :], frm[dl, :].rearrange("o h -> h o")).then_inc(node_weights, DMA)
                for g in range(NG):
                    sp.wait_ge(tab_sum, l * NG + g + 1)
                    sp.dma_start(dst_table[g * GT * NT:(g + 1) * GT * NT, :].rearrange("(i p) e -> p i e", p=NT),
                                 tab_f[0:NT, g % 2, :, EH:P]).then_inc(table_out[g % 2], DMA)
                for n in range(2, 2 * NU):
                    ids(0, n)
                if NI > 1:
                    with sp.Fori(1, NI) as i:
                        for n in range(2 * NU):
                            ids(i, n)
                for s in range(2):
                    sp.wait_ge(pick_ready[s], done(2 * (l + 1) * SU))
                    sp.sem_inc(turn, 1)
                with sp.Fori(0, n_trips) as j:
                    for u in range(GU):
                        s = u % 2
                        sp.wait_ge(g_pick_ready[s], done(nth(l * n_trips + j, u)))
                        sp.dma_start(ids_bc[:, s, 0, :], gen_rows_d[bass.ds((GU * j + u) * TPQ, TPQ), :]
                                     .rearrange("t p -> (t p)").partition_broadcast(P)).then_inc(g_ids_in[s], DMA)
                for s in range(2):
                    sp.wait_ge(g_pick_ready[s], done(nth((l + 1) * n_trips, 0)))
                    sp.sem_inc(turn, 1)
            sp.wait_ge(h_ready, (L + 1) * NB)
            sp.dma_start(x_fin[0:NT, :, :], x_v).then_inc(x_back, DMA)
            sp.wait_ge(o_ready, 1)
            sp.dma_start(out.rearrange("(i p) f -> p i f", p=NT), y[0:NT, :, :]).then_inc(stored, DMA)
            sp.wait_ge(stored, DMA)

        @block.gpsimd
        def _(pool):
            G = nc.gpsimd
            for to, pattern, b0, mult in ((lane, [[1, P]], 0, 0), (part, [[1, 1]], 0, 1), (tile_i, [[1, NB]], 0, 0),
                                          (col_no, [[1, NC]], P - NC, 0), (tile_no, [[1, T]], 0, 0)):
                G.iota(to[:, :], pattern, base=b0, channel_multiplier=mult,
                       allow_small_or_imprecise_dtypes=True).then_inc(consts, 1)
            G.memset(src_raw[:, :], N).then_inc(consts, 1)
            G.memset(dst_raw[:, :], 0).then_inc(consts, 1)
            G.memset(pads[:, :, 0], -1).then_inc(pad_set, 1)
            G.memset(pads[:, :, 1], 0).then_inc(pad_set, 1)
            pool.wait_ge(padded, DMA * -(-TT // PADT))
            with pool.Fori(0, NBAT // 2) as j:
                for s in range(2):
                    pool.wait_ge(staged[s], 3 * (j + 1))
                    pool.sem_inc(turn, 1)
                    for c in range(SB):
                        G.indirect_dma_start(
                            out=records, out_offset=bass.IndirectOffsetOnAxis(ap=pos_stage[:, s, c:c + 1], axis=0),
                            in_=rec_stage[:, s, c, :], in_offset=None).then_inc(scattered[s], DMA)
            pool.wait_ge(sorted_, 4)
            more = pool.value_load(trips[0:1, 0:1], min_val=1, max_val=NQ // GU - 1)
            n_trips = more + 1
            with pool.Fori(0, L) as l:
                def gather(trip, u, t):
                    if t == 0:
                        pool.wait_ge(g_idx_ready[u], trip + 1)
                        pool.sem_inc(turn, 1)
                    G.indirect_dma_start(
                        out=gath[:, u, t * EH:(t + 1) * EH], out_offset=None, in_=dst_table,
                        in_offset=bass.IndirectOffsetOnAxis(ap=idx_stage[:, u, t:t + 1], axis=0),
                    ).then_inc(gathered[u], DMA)

                for g in range(NG):
                    at = slice(g * GT, (g + 1) * GT)
                    pool.wait_ge(tab_mid, l * NG + g + 1)
                    G.tensor_tensor(table[0:NT, at, 2, :], tab_r1[0:NT, g % 2, :, :], table[0:NT, at, 1, :],
                                    ALU.subtract).then_inc(tab_done, 1)

                def cells(i, n):
                    tiles, s, cnt = UNITS[n % NU][1], n % 2, l * SU + i * NU + n // 2
                    pool.wait_ge(hi_ready[s], cnt + 1)
                    G.tensor_tensor(msg_r1[:, s, 0:tiles, :], msg[:, s, 0:tiles, :], msg3[:, s, 0:tiles, 0, :],
                                    ALU.subtract).then_inc(r1_ready[s], 1)
                    pool.wait_ge(mid_ready[s], cnt + 1)
                    G.tensor_tensor(msg3[:, s, 0:tiles, 2, :], msg_r1[:, s, 0:tiles, :], msg3[:, s, 0:tiles, 1, :],
                                    ALU.subtract).then_inc(msg3_ready[s], 1)

                first_trip = [(u, t) for u in range(GU) for t in range(TPQ)]
                per_unit = -(-len(first_trip) // (AHEAD * 2 * NU))
                for i in range(AHEAD):
                    for n in range(2 * NU):
                        cells(i, n)
                        for u, t in first_trip[:per_unit]:
                            gather(l * n_trips, u, t)
                        del first_trip[:per_unit]
                with pool.Fori(AHEAD, NI) as i:
                    for n in range(2 * NU):
                        cells(i, n)
                with pool.Fori(1, n_trips) as j:
                    for u in range(GU):
                        for t in range(TPQ):
                            gather(l * n_trips + j, u, t)

        @block.vector
        def _(v):
            V = nc.vector
            for s_ in (*pick_ready, *g_pick_ready, *g_added, *bucket_out, placed, tile_step, look_read, count_set):
                v.sem_inc(s_, done(0))
            v.sem_inc(ranked, groups(0))
            n_seq = [0]

            def step(ins):
                n_seq[0] += 1
                ins.then_inc(seq, 1)
                v.wait_ge(seq, n_seq[0])

            v.wait_ge(consts, N_CONSTS)
            step(V.tensor_scalar(ident[:, :], lane[:, :], part[:, 0:1], None, ALU.is_equal))
            step(V.tensor_copy(ident_b[:, :], ident[:, :]))
            step(V.tensor_scalar(tri[:, :], lane[:, :], part[:, 0:1], None, ALU.is_gt))
            step(V.memset(ones[:, :], 1.0))
            step(V.memset(ones_b[:, :], 1.0))
            step(V.memset(zeros_b[:, :], 0.0))
            step(V.tensor_scalar(pick3[:, :], lane[:, 0:3], part[:, 0:1], None, ALU.is_equal))
            step(V.memset(w2_sb[:, :], 0.0))
            step(V.memset(b1_bc[:, :], 0.0))
            step(V.memset(before[:, :, :], 0.0))
            step(V.memset(tile_end[:, :], 2.0 * T))
            step(V.memset(look[:, :, :, :], 0.0))
            step(V.tensor_scalar(before[:, 0, 0:P], lane[:, :], part[:, 0:1], None, ALU.is_lt))
            step(V.memset(before[:, 1, 0:P], 1.0))
            step(V.tensor_scalar(before[:, 1, P:2 * P], lane[:, :], part[:, 0:1], None, ALU.is_lt))

            def tile_of(to, f, tmp, size=NT):
                step(V.tensor_scalar(tmp, f, 1.0 / size, -(size - 1) / (2.0 * size), ALU.mult, ALU.add))
                step(V.tensor_scalar(to, tmp, ROUND, -ROUND, ALU.add, ALU.add))

            v.wait_ge(edges_in, DMA * 4)
            step(V.tensor_copy(tmp1[:, :], src_raw[:, :]))
            tile_of(stile[:, :], tmp1[:, :], tmp2[:, :])
            step(V.scalar_tensor_tensor(src_raw[:, :], stile[:, :], -float(NT), tmp1[:, :], ALU.mult, ALU.add))
            step(V.tensor_copy(tmp1[:, :], dst_raw[:, :]))
            tile_of(dtile[:, :], tmp1[:, :], tmp2[:, :])
            step(V.scalar_tensor_tensor(tmp2[:, :], stile[:, :], float(NB), col_no[:, :], ALU.is_equal, ALU.mult))
            step(V.scalar_tensor_tensor(cell[:, :], stile[:, :], float(NB), dtile[:, :], ALU.mult, ALU.add))
            step(V.tensor_tensor(cell[:, :], cell[:, :], tmp2[:, :], ALU.add))
            v.sem_inc(t_ready, 2)
            step(V.scalar_tensor_tensor(base[:, :], stile[:, :], float(BT * P), tmp2[:, :], ALU.mult, ALU.add))
            step(V.tensor_scalar(base[:, :], base[:, :], float((NB - 1) * C), None, ALU.add))
            step(V.tensor_tensor(room[:, :], stile[:, :], dtile[:, :], ALU.is_equal))
            step(V.tensor_scalar(room[:, :], room[:, :], float(NT), float(C), ALU.mult, ALU.add))
            for k, (t, r) in enumerate(((cell_t, NC // CB), (dtile_t, NC // CB))):
                v.wait_ge(t_done, k + 1)
                V.tensor_copy(t[:, :, :].rearrange("r b p -> r (b p)"), t_ps[0:CB, 0:r * P]).then_inc(t_copied, 1)

            def one_hots(s, at, sems):
                for oh, t in ((oh_dt, dtile), (oh_st, stile)):
                    V.tensor_tensor(oh[:, s, :, :], bc(tile_i[:, :], [P, SB, NB], 1),
                                    bc(t[:, at], [P, SB, NB], 2), ALU.is_equal).then_inc(sems[s], 1)

            with v.Fori(0, NBAT // 2) as j:
                for s in range(2):
                    v.wait_ge(c_used[s], done(j))
                    one_hots(s, bass.ds((2 * j + s) * SB, SB), c_oh)
            v.wait_ge(counted, 1)
            step(V.scalar_tensor_tensor(excess[:, :], ident[0:NB, 0:NB], -float(NT), cnt_ps, ALU.mult, ALU.add))
            V.tensor_scalar(excess[:, :], excess[:, :], -float(C), 0.0, ALU.add, ALU.max).then_inc(excess_ready, 1)
            v.wait_ge(summed, 2)
            step(V.tensor_scalar(tot_i[:, :], exc_ps[:, 0:NB], float(P - 1), None, ALU.add))
            step(V.tensor_scalar(ntile_i[:, :], tot_i[:, :], 7, None, ALU.logical_shift_right))
            step(V.tensor_copy(ntile[:, :], ntile_i[:, :]))
            step(V.tensor_tensor_scan(tile_end[:, 0:NB], ones[:, 0:NB], ntile[:, :], 0.0, ALU.mult, ALU.add))
            step(V.tensor_tensor(first[:, :], tile_end[:, 0:NB], ntile[:, :], ALU.subtract))
            step(V.tensor_scalar(first[:, :], first[:, :], float(P), float((FASTT + 1) * P - C), ALU.mult, ALU.add))
            for s in range(2):
                step(V.tensor_tensor(look[:, s, 1, :], exc_ps[0:NB, P:P + NB], first[0:NB, :], ALU.add))
                step(V.scalar_tensor_tensor(look[:, s, 1, :], ident[0:NB, 0:NB], -float(NT), look[:, s, 1, :],
                                            ALU.mult, ALU.add))
            v.sem_inc(look_ready, 1)
            step(V.tensor_scalar(trips_i[:, 0:1], tile_end[:, NB - 1:NB], float(GU * TPQ - 1), None, ALU.add))
            step(V.tensor_scalar(trips_i[:, 1:2], trips_i[:, 0:1], TRIP_BITS, None, ALU.logical_shift_right))
            step(V.tensor_scalar(trips[:, :], trips_i[:, 1:2], 2.0, -1.0, ALU.max, ALU.add))
            step(V.memset(tile_f[:, :], 0.0))

            def place(j, s):
                p = (2 * j + s) * 5
                at = bass.ds((2 * j + s) * SB, SB)
                general = r_cell[:, s, 0:SB, 1]

                def own_rank():
                    v.wait_ge(ranked, groups(2 * j + s + 1))
                    v.wait_ge(placed, done(p))
                    V.tensor_tensor(f_d[:, :], base[:, at], general, ALU.subtract)
                    V.tensor_scalar(f_v[:, :], dtile[:, at], -float(NB - 1), float(C), ALU.add, ALU.mult)
                    V.tensor_tensor(f_r[:, :], r_cell[:, s, 0:SB, 0], r_in[:, s, :], ALU.add).then_inc(placed, 1)

                def compare():
                    v.wait_ge(placed, done(p + 1))
                    V.tensor_tensor(f_m[:, :], f_r[:, :], room[:, at], ALU.is_lt)
                    V.scalar_tensor_tensor(f_t[:, :], f_r[:, :], float(C), f_v[:, :], ALU.is_lt, ALU.mult)
                    V.tensor_tensor(f_u[:, :], f_r[:, :], general, ALU.add).then_inc(placed, 1)

                def choose():
                    v.wait_ge(placed, done(p + 2))
                    V.tensor_tensor(f_m[:, :], f_m[:, :], f_d[:, :], ALU.mult)
                    V.tensor_tensor(f_u[:, :], f_u[:, :], f_t[:, :], ALU.add).then_inc(placed, 1)

                def slot():
                    v.wait_ge(placed, done(p + 3))
                    V.tensor_tensor(f_lin[:, :], f_m[:, :], f_u[:, :], ALU.add).then_inc(placed, 1)

                def parts():
                    v.wait_ge(placed, done(p + 4))
                    V.tensor_scalar(f_lo[:, :], f_lin[:, :], P - 1, None, ALU.bitwise_and)
                    V.tensor_scalar(f_hi[:, :], f_lin[:, :], 7, None, ALU.logical_shift_right).then_inc(placed, 1)

                def position():
                    v.wait_ge(placed, done(p + 5))
                    if not (isinstance(j, int) and j == 0):
                        v.wait_ge(scattered[s], DMA * SB * j)
                    V.scalar_tensor_tensor(pos_stage[:, s, :], f_lo[:, :], float(TT), f_hi[:, :],
                                           ALU.mult, ALU.add).then_inc(staged[s], 1)

                return [own_rank, compare, choose, slot, parts, position]

            def batch(j, s, behind):
                one_hots(s, bass.ds((2 * j + s) * SB, SB), oh_ready)
                v.wait_ge(bc_in[s], 2 * DMA * (j + 1))
                V.tensor_scalar(oh_d[:, s, :], dtile_bc[:, s, :], part[0:NB, 0:1], None,
                                ALU.is_equal).then_inc(oh_ready[s], 1)

                def take(g):
                    v.wait_ge(look_read, done((2 * j + s) * GPB + g + 1))
                    V.reduce_sum(r_cell[:, s, 2 * g:min(2 * g + 2, SB), :], prod[:, (s * GPB + g) % 2, 0:min(2, SB - 2 * g), :, :],
                                 AX.X).then_inc(ranked, 1)

                for g in range(GPB):
                    c0 = 2 * g
                    k = min(2, SB - c0)
                    gs = (s * GPB + g) % 2
                    n = (2 * j + s) * GPB + g
                    v.wait_ge(grouped, n + 1)
                    v.wait_ge(count_set, done(n))
                    V.tensor_tensor(look[:, 1 - gs, 0, :], look[:, gs, 0, :], group_ps[gs], ALU.add).then_inc(count_set, 1)
                    for m in range(k):
                        V.scalar_tensor_tensor(eq[:, gs, m, 0:(m + 1) * P], cell_bc[:, s, c0 * P:(c0 + m + 1) * P],
                                               cell[:, bass.ds((2 * j + s) * SB + c0 + m, 1)], before[:, m, 0:(m + 1) * P],
                                               ALU.is_equal, ALU.mult, accum_out=r_in[:, s, c0 + m:c0 + m + 1])
                    if g:
                        take(g - 1)
                    v.wait_ge(looked, n + 1)
                    V.tensor_tensor(prod[:, gs, 0:k, :, :],
                                    look_ps[:, gs, 0:k * 2 * NB].rearrange("p (c w i) -> p c w i", w=2, i=NB),
                                    bc(oh_st[:, s, c0:c0 + k, :], [P, k, 2, NB], 2), ALU.mult).then_inc(look_read, 1)
                    if behind:
                        behind.pop(0)()
                for step_ in behind:
                    step_()
                take(GPB - 1)

            def buckets_of_tiles(j):
                for k in range(ENDS):
                    v.wait_ge(tile_step, done(j * ENDS + k))
                    V.scalar_tensor_tensor(tile_f[:, :], tile_no[:, :], tile_end[:, bass.ds(j * ENDS + k, 1)],
                                           tile_f[:, :], ALU.is_ge, ALU.add).then_inc(tile_step, 1)

            for j in range(2):
                batch(j, 0, place(j - 1, 1) if j else [])
                batch(j, 1, place(j, 0))
                buckets_of_tiles(j)
            with v.Fori(2, NBAT // 2) as j:
                batch(j, 0, place(j - 1, 1))
                batch(j, 1, place(j, 0))
                buckets_of_tiles(j)
            for step_ in place(NBAT // 2 - 1, 1):
                step_()
            v.wait_ge(tile_step, done(ENDS * (NBAT // 2)))
            step(V.tensor_scalar(tile_bucket[:, :], tile_f[:, :], float(NB - 1), None, ALU.min))
            for s in range(2):
                v.wait_ge(scattered[s], DMA * (NC // 2))
            v.sem_inc(sorted_, 1)

            v.wait_ge(recs_in, DMA)

            def transposed(k, r, n):
                v.wait_ge(t_done, k)
                if k > 3:
                    v.wait_ge(t_out, DMA * (k - 3))
                V.tensor_copy(rows_t[0:r, 0:n * P], t_ps[0:r, 0:n * P]).then_inc(t_copied, 1)

            step(V.tensor_copy(recv[:, :], recs[:, 0:FASTT, 0]))
            v.sem_inc(t_ready, 1)
            step(V.tensor_copy(rf[:, :], recs[:, 0:FASTT, 1]))
            v.sem_inc(sorted_, 1)
            tile_of(rt[:, :], rf[:, :], rt[:, :])
            step(V.scalar_tensor_tensor(rb[:, :], rt[:, :], -float(NT), rf[:, :], ALU.mult, ALU.add))
            transposed(3, RBF, FASTT // RBF)
            v.sem_inc(t_ready, 1)
            v.wait_ge(recs_in, 2 * DMA)
            step(V.tensor_copy(g_recv[:, :], recs[:, 0:T, 0]))
            step(V.tensor_copy(g_dst[:, :], recs[:, 0:T, 1]))
            transposed(4, RBF, FASTT // RBF)
            v.sem_inc(t_ready, 1)
            transposed(5, RBG, T // RBG)
            v.wait_ge(t_out, 3 * DMA)
            v.sem_inc(sorted_, 2)

            step(V.memset(table[:, NB:NB + 2, :, :], 0.0))
            with v.Fori(0, L) as l:
                v.wait_ge(weights, DMA * N_WEIGHTS * (l + 1))
                B2 = 8

                def b2(k, ins):
                    ins.then_inc(b2_step, 1)
                    v.wait_ge(b2_step, l * B2 + k)

                b2(1, V.tensor_copy(b2_hi[:, :], b2_bc[:, :]))
                b2(2, V.tensor_tensor(b2_r1[:, :], b2_bc[:, :], b2_hi[:, :], ALU.subtract))
                b2(3, V.tensor_copy(b2_mid[:, :], b2_r1[:, :]))
                b2(4, V.tensor_tensor(b2_r2[:, :], b2_r1[:, :], b2_mid[:, :], ALU.subtract))
                b2(5, V.tensor_scalar(b2_sum[:, :], b2_hi[:, :], pick3[:, 0:1], None, ALU.mult))
                b2(6, V.scalar_tensor_tensor(b2_sum[:, :], b2_mid[:, :], pick3[:, 1:2], b2_sum[:, :], ALU.mult, ALU.add))
                b2(7, V.scalar_tensor_tensor(b2_sum[:, :], b2_r2[:, :], pick3[:, 2:3], b2_sum[:, :], ALU.mult, ALU.add))
                b2(8, V.tensor_copy(b2_parts[:, :, :], bc(b2_sum[:, :], [P, TPQ, EH], 1)))
                for g in range(NG + 1):
                    if g < NG:
                        s, n = g % 2, l * NG + g
                        v.wait_ge(tab_ps, n + 1)
                        if g >= 2:
                            v.wait_ge(table_out[s], DMA * (l * (NG // 2) + g // 2))
                            v.wait_ge(tab_r, n - 1)
                        V.tensor_tensor(tab_f[0:NT, s, :, :], grp_ps[s][0:NT, 0:GT * P].rearrange("p (i c) -> p i c", c=P),
                                        bc(b1_bc[0:NT, :], [NT, GT, P], 1), ALU.add).then_inc(tab_sum, 1)
                    if g:
                        s, n, at = (g - 1) % 2, l * NG + g - 1, slice((g - 1) * GT, g * GT)
                        v.wait_ge(tab_hi, n + 1)
                        if g >= 3:
                            v.wait_ge(tab_done, n - 1)
                        V.tensor_tensor(tab_r1[0:NT, s, :, :], tab_f[0:NT, s, :, :], table[0:NT, at, 0, :],
                                        ALU.subtract).then_inc(tab_r, 1)

                def cells(i, n, first=False, last=False):
                    if not last:
                        b, (u, tiles) = n // NU, UNITS[n % NU]
                        s, cnt = n % 2, l * SU + i * NU + n // 2
                        v.wait_ge(ids_in[s], 2 * DMA * (cnt + 1))
                        v.wait_ge(pre_ready[s], done(cnt))
                        for k in range(2):
                            V.tensor_scalar(pick[:, s, k, 0:tiles * P], ids_bc[:, s, k, 0:tiles * P], part[:, 0:1], None,
                                            ALU.is_equal).then_inc(pick_ready[s], 1)
                    if not (first and n < 3) and not (last and n > 2):
                        i3, n3 = unit(i, n - 3)
                        tiles, s, cnt = UNITS[n3 % NU][1], n3 % 2, l * SU + i3 * NU + n3 // 2
                        v.wait_ge(r1_ready[s], cnt + 1)
                        V.tensor_copy(msg3[:, s, 0:tiles, 1, :], msg_r1[:, s, 0:tiles, :]).then_inc(mid_ready[s], 1)
                    if not (first and n < 2) and not (last and n > 1):
                        i2, n2 = unit(i, n - 2)
                        b, (u, tiles) = n2 // NU, UNITS[n2 % NU]
                        s, cnt = n2 % 2, l * SU + i2 * NU + n2 // 2
                        v.wait_ge(agg_ready[s], done(cnt))
                        V.tensor_tensor(pick_t[:, s, 0:tiles, :], bc(lane[:, :], [P, tiles, P], 1),
                                        bc(recv[:, bass.ds((2 * i2 + b) * BT + u, tiles)], [P, tiles, P], 2),
                                        ALU.is_equal).then_inc(pick_t_ready[s], 1)
                    if not (first and n < 4) and not (last and n > 3):
                        i4, n4 = unit(i, n - 4)
                        if n4 % NU == NU - 1:
                            b = n4 // NU
                            cnt = l * SU + i4 * NU + n4 // 2
                            v.wait_ge(agg_ready[n4 % 2], done(cnt + 1))
                            V.reduce_sum(agg[:, bass.ds(2 * i4 + b, 1), :].rearrange("p o e -> p (o e)"),
                                         agg_ps[:, b, 0:3 * EH].rearrange("p (k e) -> p e k", e=EH),
                                         AX.X).then_inc(bucket_out[b], 1)

                over_units(v, cells, 4)

                more = v.value_load(trips[0:1, 0:1], min_val=1, max_val=NQ // GU - 1)
                n_trips = more + 1
                v.wait_ge(bucket_out[0], done((l + 1) * NI))
                v.wait_ge(bucket_out[1], done((l + 1) * NI))

                def prepare(q, it, s):
                    v.wait_ge(g_ids_in[s], DMA * (it + 1))
                    v.wait_ge(g_pre_ready[s], done(it))
                    V.tensor_scalar(pick[:, s, 0, :], ids_bc[:, s, 0, :], part[:, 0:1], None,
                                    ALU.is_equal).then_inc(g_pick_ready[s], 1)
                    v.wait_ge(g_agg_ready[s], done(it))
                    V.tensor_tensor(pick_g[:, s, :, :], bc(lane[:, :], [P, TPQ, P], 1),
                                    bc(g_recv[:, bass.ds(q * TPQ, TPQ)], [P, TPQ, P], 2),
                                    ALU.is_equal).then_inc(g_pick_t_ready[s], 1)

                def add(q, it, s):
                    _, bucket = nc.values_load_multi_w_load_instructions(
                        tile_bucket[0:1, bass.ds(q * TPQ, TPQ)], engines=DVE_ONLY, min_val=0, max_val=NB - 1,
                        skip_runtime_bounds_check_because="a count of buckets that end before is 0 to NB - 1")
                    v.wait_ge(g_agg_ready[s], done(it + 1))
                    for k in range(TPQ):
                        if k:
                            v.wait_ge(g_added[s], done(it * TPQ + k))
                        else:
                            v.wait_ge(g_added[1 - s], done((it + s) * TPQ))
                        where = agg[:, bass.ds(bucket[k], 1), :].rearrange("p o e -> p (o e)")
                        V.tensor_tensor(where, where, agg_ps[:, s, k * EH:(k + 1) * EH], ALU.add).then_inc(g_added[s], 1)

                for s in range(2):
                    v.wait_ge(agg_ready[s], done((l + 1) * SU))
                def units(j, more_after):
                    for u in range(GU):
                        if u + 1 < GU:
                            prepare(GU * j + u + 1, nth(l * n_trips + j, u + 1), (u + 1) % 2)
                        elif more_after:
                            prepare(GU * (j + 1), nth(l * n_trips + j + 1, 0), 0)
                        add(GU * j + u, nth(l * n_trips + j, u), u % 2)

                prepare(0, nth(l * n_trips, 0), 0)
                with v.Fori(0, more) as j:
                    units(j, True)
                units(more, False)
                for g in range(NG):
                    v.wait_ge(agg_tr, done(l * NG + g + 1))
                    V.tensor_copy(aggT[0:EH, g * GT * NT:(g + 1) * GT * NT].rearrange("p (i c) -> p i c", c=NT),
                                  grp_ps[g % 2][0:EH, 0:GT * P].rearrange("p (i c) -> p i c", c=P)[:, :, 0:NT],
                                  ).then_inc(aggT_ready, 1)
                v.wait_ge(node_weights, DMA * N_NODE_WEIGHTS * (l + 1))
                for k, (n0, w) in enumerate(CHUNKS):
                    v.wait_ge(upd_ps, l * NCH + k + 1)
                    V.scalar_tensor_tensor(hT[:, n0:n0 + w], psum[:, 6 + k % 2, 0:w], c2_sb[:, 0:1], hT[:, n0:n0 + w],
                                           ALU.add, ALU.add).then_inc(h_ready, w // NT)

            v.wait_ge(x_back, DMA)
            for g in range(NG):
                at = slice(g * GT, (g + 1) * GT)
                v.wait_ge(o_ps, g + 1)
                V.tensor_tensor(y[0:NT, at, :], grp_ps[g % 2][0:NT, 0:GT * F].rearrange("p (i f) -> p i f", f=F),
                                x_fin[0:NT, at, :], ALU.add).then_inc(o_out, 1)
            v.wait_ge(o_out, NG)
            Y, SQ, ST = y[0:NT, :, :], sq[0:NT, :, :], stat[0:NT, :, :]
            step(V.tensor_tensor(Y, Y, bc(b_out_bc[0:NT, :], [NT, NB, F], 1), ALU.add))
            step(V.reduce_sum(ST[:, 0, :], Y, AX.X))
            step(V.tensor_scalar(ST[:, 0, :], ST[:, 0, :], 1.0 / F, None, ALU.mult))
            step(V.tensor_tensor(Y, Y, bc(ST[:, 0, :], [NT, NB, F], 2), ALU.subtract))
            step(V.tensor_tensor(SQ, Y, Y, ALU.mult))
            step(V.reduce_sum(ST[:, 1, :], SQ, AX.X))
            V.tensor_scalar(ST[:, 1, :], ST[:, 1, :], 1.0 / F, 1e-5, ALU.mult, ALU.add).then_inc(fin_step, 1)
            v.wait_ge(sqrt_done, 1)
            step(V.reciprocal(ST[:, 3, :], ST[:, 2, :]))
            V.tensor_tensor(Y, Y, bc(ST[:, 3, :], [NT, NB, F], 2), ALU.mult).then_inc(o_ready, 1)

        @block.scalar
        def _(act):
            A = nc.scalar
            for s_ in (*s1_ready, *g_s1_ready, *g_msg_ready):
                act.sem_inc(s_, done(0))
            act.wait_ge(consts, N_CONSTS)
            for to, frm in ((src_raw, src), (dst_raw, dst)):
                act.dma_start(to[0:P - 1, :], frm[0:(P - 1) * NC].rearrange("(p c) -> p c", c=NC)).then_inc(edges_in, DMA)
                act.dma_start(to[P - 1:P, 0:CTAIL], frm[(P - 1) * NC:E].rearrange("(p c) -> p c", p=1)).then_inc(edges_in, DMA)
            for g in range(NG):
                s = g % 2
                act.wait_ge(x_tr, g + 1)
                if g >= 2:
                    act.wait_ge(h0_ps, g - 1)
                A.copy(xT[:, s, :].rearrange("f (i c) -> f i c", c=NT),
                       xt_ps[s][0:F, 0:GT * P].rearrange("f (i c) -> f i c", c=P)[:, :, 0:NT]).then_inc(x_tr_out, 1)
                act.wait_ge(h0_ps, g + 1)
                A.activation(hT[:, g * GT * NT:(g + 1) * GT * NT].rearrange("h (i c) -> h i c", c=NT),
                             grp_ps[s][:, 0:GT * P].rearrange("h (i c) -> h i c", c=P)[:, :, 0:NT],
                             ACT.Identity, bias=b_in_sb[:, 0:1]).then_inc(h_ready, GT)
            def batch(j, s, first_time=False):
                if not first_time:
                    act.wait_ge(scattered[s], DMA * SB * j)
                at = bass.ds((2 * j + s) * SB, SB)
                A.copy(rec_stage[:, s, :, 0], src_raw[:, at]).then_inc(staged[s], 1)
                A.copy(rec_stage[:, s, :, 1], dst_raw[:, at]).then_inc(staged[s], 1)

            act.wait_ge(look_ready, 1)
            for s in range(2):
                batch(0, s, first_time=True)
            with act.Fori(1, NBAT // 2) as j:
                for s in range(2):
                    batch(j, s)
            act.wait_ge(sorted_, 4)
            more = act.value_load(trips[0:1, 0:1], min_val=1, max_val=NQ // GU - 1)
            n_trips = more + 1
            with act.Fori(0, L) as l:
                for g in range(NG + 1):
                    if g < NG:
                        act.wait_ge(tab_sum, l * NG + g + 1)
                        A.copy(table[0:NT, g * GT:(g + 1) * GT, 0, :], tab_f[0:NT, g % 2, :, :]).then_inc(tab_hi, 1)
                    if g:
                        act.wait_ge(tab_r, l * NG + g)
                        A.copy(table[0:NT, (g - 1) * GT:g * GT, 1, :], tab_r1[0:NT, (g - 1) % 2, :, :]).then_inc(tab_mid, 1)
                def stage_indices(j, u):
                    A.copy(idx_stage[:, u, :], g_dst[:, bass.ds((GU * j + u) * TPQ, TPQ)]).then_inc(g_idx_ready[u], 1)

                for s in range(2):
                    act.wait_ge(table_out[s], DMA * (NG // 2) * (l + 1))
                for u in range(GU):
                    stage_indices(0, u)
                act.wait_ge(tab_done, (l + 1) * NG)

                def bucket_rows(i, b):
                    A.copy(rows[0:NT, b, :, :], table[0:NT, bass.ds(2 * i + b, 1), :, :]
                           .rearrange("p o k e -> p (o k) e")).then_inc(rows_ready[b], 1)

                def cells(i, n, first=False, last=False):
                    if not last:
                        s, cnt = n % 2, l * SU + i * NU + n // 2
                        tiles = UNITS[n % NU][1]
                        act.wait_ge(pre_ready[s], done(cnt + 1))
                        act.wait_ge(z_ready[s], done(cnt))
                        A.activation(s1[:, s, 0:tiles // 2 * P], pre_ps[:, s, 0:tiles // 2 * P],
                                     ACT.Silu).then_inc(s1_ready[s], 1)
                        if n % NU == NU - 1:
                            bucket_rows(i + 1, n // NU)
                    if not (first and n < 1) and not (last and n > 0):
                        i1, n1 = unit(i, n - 1)
                        tiles, s, cnt = UNITS[n1 % NU][1], n1 % 2, l * SU + i1 * NU + n1 // 2
                        act.wait_ge(z_ready[s], done(cnt + 1))
                        act.wait_ge(agg_ready[s], done(cnt))
                        A.activation(msg[:, s, 0:tiles, :].rearrange("p t e -> p (t e)"), z_ps[:, s, 0:tiles * EH],
                                     ACT.Silu).then_inc(msg_set, 1)
                        m1 = l * 2 * SU + i1 * 2 * NU + n1
                        act.wait_ge(msg_set, m1 + 1)
                        A.copy(msg3[:, s, 0:tiles, 0, :], msg[:, s, 0:tiles, :]).then_inc(hi_ready[s], 1)

                for b in range(2):
                    bucket_rows(0, b)
                over_units(act, cells, 1)

                def stage_rows(q, s):
                    _, bucket = nc.values_load_multi_w_load_instructions(
                        tile_bucket[0:1, bass.ds(q * TPQ, TPQ)], engines=ACT_ONLY, min_val=0, max_val=NB - 1,
                        skip_runtime_bounds_check_because="a count of buckets that end before is 0 to NB - 1")
                    for k in range(TPQ):
                        A.copy(rows_g[0:NT, s, k, :, :],
                               table[0:NT, bass.ds(bucket[k], 1), :, 0:EH].rearrange("p o k e -> p (o k) e"),
                               ).then_inc(g_rows_ready[s], 1)

                def units(j, more_after):
                    for u in range(GU):
                        s, it = u % 2, nth(l * n_trips + j, u)
                        act.wait_ge(g_pre_ready[s], done(it + 1))
                        act.wait_ge(g_z_ready[s], done(it))
                        A.activation(s1[:, s, :], pre_ps[:, s, :], ACT.Silu).then_inc(g_s1_ready[s], 1)
                        if more_after:
                            stage_indices(j + 1, u)
                        act.wait_ge(g_z_ready[s], done(it + 1))
                        act.wait_ge(g_agg_ready[s], done(it))
                        A.activation(msg[:, s, :, :].rearrange("p t e -> p (t e)"), z_ps[:, s, :],
                                     ACT.Silu).then_inc(g_msg_ready[s], 1)
                        if more_after or u + 2 < GU:
                            stage_rows(GU * j + u + 2, s)

                for s in range(2):
                    stage_rows(s, s)
                for s in range(2):
                    act.wait_ge(agg_ready[s], done((l + 1) * SU))
                with act.Fori(0, more) as j:
                    units(j, True)
                units(more, False)
                act.wait_ge(node_weights, DMA * N_NODE_WEIGHTS * (l + 1))
                for k, (n0, w) in enumerate(CHUNKS):
                    act.wait_ge(u_ps_ready, l * NCH + k + 1)
                    if k >= 2:
                        act.wait_ge(upd_ps, l * NCH + k - 1)
                    A.activation(u_sb[:, k % 2, 0:w], psum[:, 4 + k % 2, 0:w], ACT.Silu,
                                 bias=c1_sb[:, 0:1]).then_inc(u_ready, 1)
            act.wait_ge(fin_step, 1)
            A.activation(stat[0:NT, 2, :], stat[0:NT, 1, :], ACT.Sqrt).then_inc(sqrt_done, 1)

        @block.tensor
        def _(pe):
            def mm(o, a, b, start=True, stop=True):
                return nc.tensor.matmul(o, a, b, start=start, stop=stop)

            for s_ in (*pre_ready, *z_ready, *agg_ready, *g_pre_ready, *g_z_ready, *g_agg_ready, agg_tr,
                       *c_used):
                pe.sem_inc(s_, done(0))
            pe.wait_ge(seq, 15)
            pe.wait_ge(loaded, DMA * 5)
            for g in range(NG):
                s = g % 2
                if g >= 2:
                    pe.wait_ge(h_ready, (g - 1) * GT)
                for i in range(GT):
                    last = mm(xt_ps[s][0:F, i * P:i * P + NT], x_sb[0:NT, g * GT + i, :], ident[0:NT, 0:NT])
                last.then_inc(x_tr, 1)
                pe.wait_ge(x_tr_out, g + 1)
                for i in range(GT):
                    last = mm(grp_ps[s][:, i * P:i * P + NT], W_in_sb[:, :], xT[:, s, i * NT:(i + 1) * NT])
                last.then_inc(h0_ps, 1)
            pe.wait_ge(h_ready, NB)

            def transpose(k, a, r, n, i):
                pe.wait_ge(t_ready, k)
                if k > 1:
                    pe.wait_ge(t_copied, k - 1)
                for m in range(n):
                    last = mm(t_ps[0:r, m * P:(m + 1) * P], a[:, m * r:(m + 1) * r], i[:, :])
                last.then_inc(t_done, 1)

            transpose(1, cell, CB, NC // CB, ident)
            pe.wait_ge(t_copied, 1)
            for m in range(NC // CB):
                last = mm(t_ps[0:CB, m * P:(m + 1) * P], dtile[:, m * CB:(m + 1) * CB], ident_b[:, :])
            last.then_inc(t_done, 1)
            Z = zeros_b[:, 0:NB]
            mm(cnt_ps, Z, Z, stop=False)
            with pe.Fori(0, NBAT // 2) as j:
                for s in range(2):
                    pe.wait_ge(c_oh[s], 2 * (j + 1))
                    for c in range(SB):
                        last = mm(cnt_ps, oh_dt[:, s, c, :], oh_st[:, s, c, :], start=False, stop=False)
                    last.then_inc(c_used[s], 1)
            mm(cnt_ps, Z, Z, start=False).then_inc(counted, 1)
            pe.wait_ge(excess_ready, 1)
            mm(exc_ps[:, 0:NB], ones[0:NB, :], excess[:, :]).then_inc(summed, 1)
            mm(exc_ps[0:NB, P:P + NB], tri[0:NB, 0:NB], excess[:, :]).then_inc(summed, 1)
            pe.wait_ge(look_ready, 1)
            with pe.Fori(0, NBAT // 2) as j:
                for s in range(2):
                    pe.wait_ge(oh_ready[s], 3 * (j + 1))
                    for g in range(GPB):
                        c0 = 2 * g
                        k = min(2, SB - c0)
                        gs = (s * GPB + g) % 2
                        n = (2 * j + s) * GPB + g
                        for m in range(k):
                            last = mm(group_ps[gs], oh_dt[:, s, c0 + m, :], oh_st[:, s, c0 + m, :],
                                      start=m == 0, stop=m == k - 1)
                        last.then_inc(grouped, 1)
                        pe.wait_ge(count_set, done(n))
                        pe.wait_ge(look_read, n if s + g else done(n))
                        for m in range(k):
                            last = mm(look_ps[:, gs, m * 2 * NB:(m + 1) * 2 * NB], oh_d[:, s, (c0 + m) * P:(c0 + m + 1) * P],
                                      look[:, gs, :, :].rearrange("p w i -> p (w i)"))
                        last.then_inc(looked, 1)
            transpose(3, recv, RBF, FASTT // RBF, ident_b)
            transpose(4, rb, RBF, FASTT // RBF, ident_b)
            transpose(5, g_recv, RBG, T // RBG, ident_b)
            pe.wait_ge(sorted_, 4)

            with pe.Fori(0, L) as l:
                pe.wait_ge(weights, DMA * N_WEIGHTS * (l + 1))
                for g in range(NG):
                    pe.wait_ge(h_ready, l * NB + (g + 1) * GT)
                    if g >= 2:
                        pe.wait_ge(tab_sum, l * NG + g - 1)
                    for i in range(GT):
                        n = g * GT + i
                        last = mm(grp_ps[g % 2][0:NT, i * P:(i + 1) * P], hT[:, n * NT:(n + 1) * NT], w1_sb[:, :])
                    last.then_inc(tab_ps, 1)
                pe.wait_ge(tab_done, (l + 1) * NG)
                pe.wait_ge(b2_step, 8 * (l + 1))

                def before_silu(i, n):
                    b, (u, tiles) = n // NU, UNITS[n % NU]
                    s, cnt, half = n % 2, l * SU + i * NU + n // 2, tiles // 2 * P
                    pe.wait_ge(s1_ready[s], done(cnt))
                    pe.wait_ge(pick_ready[s], done(2 * (cnt + 1)))
                    pe.wait_ge(rows_ready[b], l * (NI + 1) + i + 1)
                    at = pieces(tiles, u)
                    ends = {h: max(k for k, p in enumerate(at) if p[0] == h) for h in range(2)
                            if any(p[0] == h for p in at)}
                    for k in range(3):
                        for h in range(2):
                            mm(pre_ps[h * EH:(h + 1) * EH, s, 0:half], rows[0:NT, b, k, 0:EH],
                               pick[0:NT, s, 0, h * half:(h + 1) * half], start=k == 0, stop=k == 2 and h not in ends)
                    for m, (h, c0, w, d) in enumerate(at):
                        for k in range(3):
                            last = mm(pre_ps[h * EH:(h + 1) * EH, s, c0:c0 + w],
                                      table[0:NT, d, k, EH:P] if d < NB else rows[0:NT, b, k, EH:P],
                                      pick[0:NT, s, 1, h * half + c0:h * half + c0 + w],
                                      start=False, stop=k == 2 and m == ends[h])
                    last.then_inc(pre_ready[s], 1)

                def second(i, n):
                    tiles, s, cnt = UNITS[n % NU][1], n % 2, l * SU + i * NU + n // 2
                    pe.wait_ge(s1_ready[s], done(cnt + 1))
                    mm(z_ps[:, s, 0:tiles * EH], ones_b[:, :],
                       b2_parts[:, 0:tiles, :].rearrange("p t e -> p (t e)"), stop=False)
                    for k in range(tiles // 2):
                        last = mm(z_ps[:, s, k * P:(k + 1) * P], s1[:, s, k * P:(k + 1) * P], w2_sb[:, :],
                                  start=False, stop=k == tiles // 2 - 1)
                    last.then_inc(z_ready[s], 1)

                def sums(i, n):
                    b, (u, tiles) = n // NU, UNITS[n % NU]
                    s, cnt = n % 2, l * SU + i * NU + n // 2
                    pe.wait_ge(pick_t_ready[s], cnt + 1)
                    pe.wait_ge(msg3_ready[s], cnt + 1)
                    if u == 0:
                        pe.wait_ge(bucket_out[b], done(l * NI + i))
                    for m in range(tiles):
                        t = m // 2 + (m % 2) * (tiles // 2)
                        last = mm(agg_ps[:, b, 0:3 * EH], pick_t[:, s, t, :],
                                  msg3[:, s, m, :, :].rearrange("p k e -> p (k e)"),
                                  start=u + m == 0, stop=u + m == BT - 1)
                    last.then_inc(agg_ready[s], 1)

                def cells(i, n, first=False, last=False):
                    if not last:
                        before_silu(i, n)
                    if not (first and n < 3):
                        sums(*unit(i, n - 3))
                    if not (first and n < 1) and not (last and n > 0):
                        second(*unit(i, n - 1))

                over_units(pe, cells, 3)

                more = pe.value_load(trips[0:1, 0:1], min_val=1, max_val=NQ // GU - 1)
                n_trips = more + 1
                for s in range(2):
                    pe.wait_ge(s1_ready[s], done((l + 1) * SU))
                    pe.wait_ge(bucket_out[s], done((l + 1) * NI))
                pe.sem_inc(turn, 1)
                with pe.Fori(0, n_trips) as j:
                    for u in range(GU):
                        s, it = u % 2, nth(l * n_trips + j, u)
                        pe.wait_ge(gathered[u], DMA * TPQ * (l * n_trips + j + 1))
                        pe.wait_ge(g_s1_ready[s], done(it))
                        for k in range(PPQ):
                            mm(pre_ps[:, s, k * P:(k + 1) * P], gath[:, u, k * P:(k + 1) * P], ident[:, :],
                               start=k == 0, stop=False)
                        pe.wait_ge(g_pick_ready[s], done(it + 1))
                        pe.wait_ge(g_rows_ready[s], TPQ * (it + 1))
                        for k in range(PPQ):
                            for p3 in range(3):
                                for h in range(2):
                                    t = 2 * k + h
                                    last = mm(pre_ps[h * EH:(h + 1) * EH, s, k * P:(k + 1) * P],
                                              rows_g[0:NT, s, t, p3, :], pick[0:NT, s, 0, t * P:(t + 1) * P],
                                              start=False, stop=k == PPQ - 1 and p3 == 2)
                        last.then_inc(g_pre_ready[s], 1)
                        pe.wait_ge(g_msg_ready[s], done(it))
                        mm(z_ps[:, s, :], ones_b[:, :], b2_parts[:, :, :].rearrange("p t e -> p (t e)"), stop=False)
                        pe.wait_ge(g_s1_ready[s], done(it + 1))
                        for k in range(PPQ):
                            last = mm(z_ps[:, s, k * P:(k + 1) * P], s1[:, s, k * P:(k + 1) * P], w2_sb[:, :],
                                      start=False, stop=k == PPQ - 1)
                        last.then_inc(g_z_ready[s], 1)
                        pe.wait_ge(g_added[s], done(TPQ * it))
                        pe.wait_ge(g_pick_t_ready[s], it + 1)
                        pe.wait_ge(g_msg_ready[s], done(it + 1))
                        for t in range(TPQ):
                            last = mm(agg_ps[:, s, t * EH:(t + 1) * EH], pick_g[:, s, t, :], msg[:, s, t, :])
                        last.then_inc(g_agg_ready[s], 1)
                for s in range(2):
                    pe.wait_ge(g_added[s], done(TPQ * nth(n_trips * (l + 1), 0)))
                for g in range(NG):
                    if g >= 2:
                        pe.wait_ge(aggT_ready, l * NG + g - 1)
                    for i in range(GT):
                        last = mm(grp_ps[g % 2][0:EH, i * P:i * P + NT], agg[0:NT, g * GT + i, :], ident[0:NT, 0:NT])
                    last.then_inc(agg_tr, 1)
                pe.wait_ge(aggT_ready, (l + 1) * NG)
                pe.wait_ge(node_weights, DMA * N_NODE_WEIGHTS * (l + 1))
                for k in range(NCH + 1):
                    if k < NCH:
                        (n0, w), at = CHUNKS[k], psum[:, 4 + k % 2, 0:CHUNKS[k][1]]
                        if k >= 2:
                            pe.wait_ge(u_ready, l * NCH + k - 1)
                        mm(at, m1h_sb[:, :], hT[:, n0:n0 + w], stop=False)
                        mm(at, m1a_sb[:, :], aggT[0:EH, n0:n0 + w], start=False).then_inc(u_ps_ready, 1)
                    if k:
                        n0, w = CHUNKS[k - 1]
                        pe.wait_ge(u_ready, l * NCH + k)
                        if k >= 3:
                            pe.wait_ge(h_ready, (l + 1) * NB + CHUNKS[k - 2][0] // NT)
                        mm(psum[:, 6 + (k - 1) % 2, 0:w], m2_sb[:, :], u_sb[:, (k - 1) % 2, 0:w]).then_inc(upd_ps, 1)
            pe.wait_ge(h_ready, (L + 1) * NB)
            for g in range(NG):
                if g >= 2:
                    pe.wait_ge(o_out, g - 1)
                for i in range(GT):
                    n = g * GT + i
                    last = mm(grp_ps[g % 2][0:NT, i * F:(i + 1) * F], hT[:, n * NT:(n + 1) * NT], W_out_sb[:, :])
                last.then_inc(o_ps, 1)


_INS = ['x', 'src', 'dst'] + ['L0_gnn_' + n for n in
                              ('W_in', 'b_in', 'eW1', 'eb1', 'eW2', 'eb2', 'nW1', 'nb1', 'nW2', 'nb2', 'W_out', 'b_out')]


def kernel(**inputs):
    import numpy as _np
    import concourse.bacc as _bacc
    from concourse import mybir as _mybir
    from concourse.bass_utils import run_bass_kernel_spmd as _run

    nc = _bacc.Bacc("TRN2", target_bir_lowering=False, num_devices=1)
    arrays, args = {}, []
    for name in _INS:
        a = _np.ascontiguousarray(inputs[name])
        arrays[f"in_{name}_dram"] = a
        args.append(nc.dram_tensor(f"in_{name}_dram", a.shape, _mybir.dt.from_np(a.dtype), kind="ExternalInput").ap())
    shape = tuple(arrays["in_x_dram"].shape)
    args.append(nc.dram_tensor("out_dram", shape, _mybir.dt.float32, kind="ExternalOutput").ap())
    build_gnn(nc, *args)
    r = _run(nc, [arrays], core_ids=[0])
    return r.results[0]["out_dram"]
```
